# Optimizing a Trainium2 kernel written in Bass

```python
import numpy as np
import jax
import jax.numpy as jnp

def _softmax(x, axis=-1):
    return jax.nn.softmax(x, axis=axis)

def _gelu(x):
    return jax.nn.gelu(x, approximate=True)

def _silu(x):
    return jax.nn.silu(x)

def _sigmoid(x):
    return jax.nn.sigmoid(x)

def _layernorm(x, axis=-1, eps=1e-05):
    m = jnp.mean(x, axis=axis, keepdims=True)
    v = jnp.var(x, axis=axis, keepdims=True)
    return (x - m) / jnp.sqrt(v + eps)

def _scatter_add(tgt, idx, src, axis=0):
    return tgt.at[idx].add(src)

def _segment_sum(src, seg, n):
    return jax.ops.segment_sum(src, seg, n)
kernel_name = 'mk_perceiver_d1_seqx_r4_abc581'

def setup_inputs(seed: int=0):
    np.random.seed(seed)
    _w = jnp.asarray

    def _rec_inputs():
        import jax
        import jax.numpy as jnp
        _rk = jax.random.key(seed)
        x = -0.0002928 + 1 * jax.random.normal(jax.random.fold_in(_rk, 1), (1, 256, 512), jnp.float32)
        _lenS = 256 - jax.random.randint(jax.random.fold_in(_rk, 7), (1,), 0, max(1, 256 // 4) + 1, jnp.int32)
        _lenS2 = 4096 - jax.random.randint(jax.random.fold_in(_rk, 8), (1,), 0, max(1, 4096 // 4) + 1, jnp.int32)
        _ctx_512P = jax.random.normal(jax.random.fold_in(_rk, 11), (1, 16, 128), jnp.float32)
        _ctx_512c = jax.random.dirichlet(jax.random.fold_in(_rk, 511), 0.3 * jnp.ones((16,), jnp.float32), (1, 4096))
        _ctx_512t = jnp.einsum('bsk,bkd->bsd', _ctx_512c, _ctx_512P)
        _ctx_512t = _ctx_512t * jax.lax.rsqrt(jnp.mean(jnp.square(_ctx_512t)) + 1e-12) * 0.953939
        ctx_512 = 0.000227908 + 0.99994 * (_ctx_512t + 0.3 * jax.random.normal(jax.random.fold_in(_rk, 611), (1, 4096, 128), jnp.float32))
        return (x, ctx_512)
    x, ctx_512 = _rec_inputs()

    def _L0_xattn_setup():
        import jax, jax.numpy as jnp
        import numpy as np
        B, S, L = (2, 256, 256)
        DIM_Q, H, K, D_C, D_CQ, R = (512, 16, 128, 128, 384, 64)

        def _rope_tables(seq_len, dim, dtype):
            inv_freq = 1.0 / 10000.0 ** (jnp.arange(0, dim, 2, dtype=dtype) / dim)
            t = jnp.arange(seq_len, dtype=dtype)
            freqs = t[:, None] * inv_freq[None, :]
            sin = jnp.repeat(jnp.sin(freqs), 2, axis=-1)
            cos = jnp.repeat(jnp.cos(freqs), 2, axis=-1)
            return (sin, cos)

        def _rotate_half(x):
            h = x.shape[-1] // 2
            return jnp.concatenate([-x[..., h:], x[..., :h]], axis=-1)
        key = jax.random.key(seed)
        ks = jax.random.split(key, 8)
        s_in = 1.0 / np.sqrt(DIM_Q)
        s_k = 1.0 / np.sqrt(K)
        s_cq = 1.0 / np.sqrt(D_CQ)
        s_c = 1.0 / np.sqrt(D_C)
        return {'hidden_q': jax.random.normal(ks[0], (B, S, DIM_Q), jnp.float32), 'kv_c': jax.random.normal(ks[1], (B, L, D_C), jnp.float32), 'Wq': jax.random.normal(ks[2], (H * K, DIM_Q), jnp.float32) * s_in, 'w_kc_q': jax.random.normal(ks[3], (H, K, D_CQ), jnp.float32) * s_k, 'w_kc_kv': jax.random.normal(ks[4], (H, K, D_C), jnp.float32) * s_k, 'W_qr': jax.random.normal(ks[5], (H, D_CQ, R), jnp.float32) * s_cq / np.sqrt(R), 'W_kr': jax.random.normal(ks[6], (H, D_C, R), jnp.float32) * s_c, 'Wo': jax.random.normal(ks[7], (DIM_Q, H * K), jnp.float32) * s_k}
    _L0_xattn_all = _L0_xattn_setup()
    _L0_xattn_in = {k: v for k, v in _L0_xattn_all.items() if k in ('Wq', 'w_kc_q', 'w_kc_kv', 'W_qr', 'W_kr', 'Wo')}
    del _L0_xattn_all

    def _L0_attn_setup():
        import jax, jax.numpy as jnp
        import numpy as np
        EMBED_DIM = 512
        NUM_HEADS = 16
        Q_LORA = 128
        KV_LORA = 128
        ROPE_DIM = 64
        NOPE_DIM = EMBED_DIM // NUM_HEADS
        V_DIM = EMBED_DIM // NUM_HEADS
        Q_HEAD_DIM = NOPE_DIM + ROPE_DIM
        BASE = 10000.0

        def rope(x, offset=0, base=BASE):
            b, n, h, d = x.shape
            inv_freq = base ** (-jnp.arange(0, d, 2, dtype=jnp.float32) / d)
            pos = jnp.arange(offset, offset + n, dtype=jnp.float32)
            ang = pos[:, None] * inv_freq[None, :]
            cos = jnp.cos(ang)[None, :, None, :]
            sin = jnp.sin(ang)[None, :, None, :]
            x1 = x[..., 0::2]
            x2 = x[..., 1::2]
            o1 = x1 * cos - x2 * sin
            o2 = x1 * sin + x2 * cos
            return jnp.stack([o1, o2], axis=-1).reshape(b, n, h, d)
        key = jax.random.key(seed)
        ks = jax.random.split(key, 6)
        s = 0.02
        x = jax.random.normal(ks[0], (2, 512, EMBED_DIM), dtype=jnp.float32)
        Wqa = jax.random.normal(ks[1], (EMBED_DIM, Q_LORA), dtype=jnp.float32) * s
        Wqb = jax.random.normal(ks[2], (Q_LORA, NUM_HEADS * Q_HEAD_DIM), dtype=jnp.float32) * s
        Wkva = jax.random.normal(ks[3], (EMBED_DIM, KV_LORA + ROPE_DIM), dtype=jnp.float32) * s
        Wkvb = jax.random.normal(ks[4], (KV_LORA, NUM_HEADS * (NOPE_DIM + V_DIM)), dtype=jnp.float32) * s
        Wo = jax.random.normal(ks[5], (NUM_HEADS * V_DIM, EMBED_DIM), dtype=jnp.float32) * s
        return {'x': x, 'Wqa': Wqa, 'Wqb': Wqb, 'Wkva': Wkva, 'Wkvb': Wkvb, 'Wo': Wo}
    _L0_attn_all = _L0_attn_setup()
    _L0_attn_in = {k: v for k, v in _L0_attn_all.items() if k in ('Wqa', 'Wqb', 'Wkva', 'Wkvb', 'Wo')}
    del _L0_attn_all

    def _L0_ffn_setup():
        import math
        import jax, jax.numpy as jnp
        import numpy as np
        from jax import lax
        D = 512
        I = 256
        E = 32
        K = 4
        NG = 8
        TKG = 3
        NSH = 2
        SCALE = 2.5
        CF = 1.25
        B, S = (2, 512)

        def _router(x, router_w, e_bias):
            scores = jax.nn.sigmoid(x @ router_w.T)
            sc = scores + e_bias[None, :]
            T = x.shape[0]
            gs = sc.reshape(T, NG, E // NG)
            group_scores = lax.top_k(gs, 2)[0].sum(-1)
            _, gidx = lax.top_k(group_scores, TKG)
            gmask = jnp.zeros((T, NG), sc.dtype).at[jnp.arange(T)[:, None], gidx].set(1.0)
            smask = jnp.repeat(gmask, E // NG, axis=1)
            masked = jnp.where(smask > 0, sc, 0.0)
            _, topk_idx = lax.top_k(masked, K)
            topk_w = jnp.take_along_axis(scores, topk_idx, axis=1)
            topk_w = topk_w / (topk_w.sum(-1, keepdims=True) + 1e-20)
            topk_w = topk_w * SCALE
            return (topk_idx.astype(jnp.int32), topk_w)

        def _moe_forward(hidden_states, router_w, e_bias, W_gate, W_up, W_down, shared_gate, shared_up, shared_down):
            b, s, d = hidden_states.shape
            T = b * s
            C = int(math.ceil(CF * T / E))
            EC = E * C
            x = hidden_states.reshape(T, d)
            topk_idx, topk_w = _router(x, router_w, e_bias)
            expert_flat = topk_idx.reshape(-1)
            w_flat = topk_w.reshape(-1)
            tok_flat = jnp.repeat(jnp.arange(T, dtype=jnp.int32), K)
            sort_ix = jnp.argsort(expert_flat)
            e_sorted = expert_flat[sort_ix]
            tok_s = tok_flat[sort_ix]
            w_s = w_flat[sort_ix]
            counts = jnp.zeros(E, jnp.int32).at[e_sorted].add(1)
            group_start = jnp.concatenate([jnp.zeros(1, jnp.int32), jnp.cumsum(counts)[:-1].astype(jnp.int32)])
            pos = jnp.arange(T * K, dtype=jnp.int32) - group_start[e_sorted]
            valid = pos < C
            dest = e_sorted * C + jnp.where(valid, pos, 0)
            slots_token = jnp.zeros(EC, jnp.int32).at[dest].add(jnp.where(valid, tok_s, 0))
            slots_w = jnp.zeros(EC, w_s.dtype).at[dest].add(jnp.where(valid, w_s, 0.0))
            Xp = x[slots_token].reshape(E, C, d)
            G = jnp.einsum('ecd,edi->eci', Xp, W_gate)
            U = jnp.einsum('ecd,edi->eci', Xp, W_up)
            Y = jnp.einsum('eci,eid->ecd', jax.nn.silu(G) * U, W_down)
            Yf = Y.reshape(EC, d) * slots_w[:, None]
            out = jnp.zeros((T, d), x.dtype).at[slots_token].add(Yf)
            shared = jax.nn.silu(x @ shared_gate.T) * (x @ shared_up.T) @ shared_down.T
            return (out + shared).reshape(b, s, d)
        key = jax.random.key(seed)
        ks = jax.random.split(key, 8)

        def rn(k, shape, scale=0.02):
            return jax.random.normal(k, shape, jnp.float32) * scale
        return {'hidden_states': jax.random.normal(ks[0], (B, S, D), jnp.float32), 'router_w': rn(ks[1], (E, D)), 'e_bias': jnp.zeros((E,), jnp.float32), 'W_gate': rn(ks[2], (E, D, I)), 'W_up': rn(ks[3], (E, D, I)), 'W_down': rn(ks[4], (E, I, D)), 'shared_gate': rn(ks[5], (I * NSH, D)), 'shared_up': rn(ks[6], (I * NSH, D)), 'shared_down': rn(ks[7], (D, I * NSH))}
    _L0_ffn_all = _L0_ffn_setup()
    _L0_ffn_in = {k: v for k, v in _L0_ffn_all.items() if k in ('router_w', 'e_bias', 'W_gate', 'W_up', 'W_down', 'shared_gate', 'shared_up', 'shared_down')}
    del _L0_ffn_all
    return {'x': x, 'ctx_512': ctx_512, 'L0_xattn_Wq': _L0_xattn_in['Wq'], 'L0_xattn_w_kc_q': _L0_xattn_in['w_kc_q'], 'L0_xattn_w_kc_kv': _L0_xattn_in['w_kc_kv'], 'L0_xattn_W_qr': _L0_xattn_in['W_qr'], 'L0_xattn_W_kr': _L0_xattn_in['W_kr'], 'L0_xattn_Wo': _L0_xattn_in['Wo'], 'L0_attn_Wqa': _L0_attn_in['Wqa'], 'L0_attn_Wqb': _L0_attn_in['Wqb'], 'L0_attn_Wkva': _L0_attn_in['Wkva'], 'L0_attn_Wkvb': _L0_attn_in['Wkvb'], 'L0_attn_Wo': _L0_attn_in['Wo'], 'L0_ffn_router_w': _L0_ffn_in['router_w'], 'L0_ffn_e_bias': _L0_ffn_in['e_bias'], 'L0_ffn_W_gate': _L0_ffn_in['W_gate'], 'L0_ffn_W_up': _L0_ffn_in['W_up'], 'L0_ffn_W_down': _L0_ffn_in['W_down'], 'L0_ffn_shared_gate': _L0_ffn_in['shared_gate'], 'L0_ffn_shared_up': _L0_ffn_in['shared_up'], 'L0_ffn_shared_down': _L0_ffn_in['shared_down']}

def reference(x, ctx_512, L0_xattn_Wq, L0_xattn_w_kc_q, L0_xattn_w_kc_kv, L0_xattn_W_qr, L0_xattn_W_kr, L0_xattn_Wo, L0_attn_Wqa, L0_attn_Wqb, L0_attn_Wkva, L0_attn_Wkvb, L0_attn_Wo, L0_ffn_router_w, L0_ffn_e_bias, L0_ffn_W_gate, L0_ffn_W_up, L0_ffn_W_down, L0_ffn_shared_gate, L0_ffn_shared_up, L0_ffn_shared_down):
    import jax
    import jax.numpy as jnp

    def _L0_xattn_ref(hidden_q, kv_c, Wq, w_kc_q, w_kc_kv, W_qr, W_kr, Wo):
        import jax, jax.numpy as jnp
        import numpy as np
        B, S, L = (2, 256, 256)
        DIM_Q, H, K, D_C, D_CQ, R = (512, 16, 128, 128, 384, 64)

        def _rope_tables(seq_len, dim, dtype):
            inv_freq = 1.0 / 10000.0 ** (jnp.arange(0, dim, 2, dtype=dtype) / dim)
            t = jnp.arange(seq_len, dtype=dtype)
            freqs = t[:, None] * inv_freq[None, :]
            sin = jnp.repeat(jnp.sin(freqs), 2, axis=-1)
            cos = jnp.repeat(jnp.cos(freqs), 2, axis=-1)
            return (sin, cos)

        def _rotate_half(x):
            h = x.shape[-1] // 2
            return jnp.concatenate([-x[..., h:], x[..., :h]], axis=-1)
        b, s, _ = hidden_q.shape
        l = kv_c.shape[1]
        q_hk = (hidden_q @ Wq.T).reshape(b, s, H, K)
        q_big = jnp.einsum('bshk,hkq->bshq', q_hk, w_kc_q)
        sin, cos = _rope_tables(l, D_C, kv_c.dtype)
        kv_rope = kv_c * cos[None] + _rotate_half(kv_c) * sin[None]
        q_r = jnp.einsum('bshq,hqr->bhsr', q_big, W_qr)
        k_r = jnp.einsum('bld,hdr->bhlr', kv_rope, W_kr)
        scores = jnp.einsum('bhsr,bhlr->bhsl', q_r, k_r)
        attn = jax.nn.softmax(scores, axis=-1)
        ctx_c = jnp.einsum('bhsl,bld->bhsd', attn, kv_rope)
        ctx_lat = jnp.einsum('bhsd,hkd->bshk', ctx_c, w_kc_kv)
        out = ctx_lat.reshape(b, s, H * K) @ Wo.T
        return out

    def _L0_attn_ref(x, Wqa, Wqb, Wkva, Wkvb, Wo):
        import jax, jax.numpy as jnp
        import numpy as np
        EMBED_DIM = 512
        NUM_HEADS = 16
        Q_LORA = 128
        KV_LORA = 128
        ROPE_DIM = 64
        NOPE_DIM = EMBED_DIM // NUM_HEADS
        V_DIM = EMBED_DIM // NUM_HEADS
        Q_HEAD_DIM = NOPE_DIM + ROPE_DIM
        BASE = 10000.0

        def rope(x, offset=0, base=BASE):
            b, n, h, d = x.shape
            inv_freq = base ** (-jnp.arange(0, d, 2, dtype=jnp.float32) / d)
            pos = jnp.arange(offset, offset + n, dtype=jnp.float32)
            ang = pos[:, None] * inv_freq[None, :]
            cos = jnp.cos(ang)[None, :, None, :]
            sin = jnp.sin(ang)[None, :, None, :]
            x1 = x[..., 0::2]
            x2 = x[..., 1::2]
            o1 = x1 * cos - x2 * sin
            o2 = x1 * sin + x2 * cos
            return jnp.stack([o1, o2], axis=-1).reshape(b, n, h, d)
        b, n, d = x.shape
        h = NUM_HEADS
        q = x @ Wqa @ Wqb
        q = q.reshape(b, n, h, Q_HEAD_DIM)
        q_nope, q_pe = (q[..., :NOPE_DIM], q[..., NOPE_DIM:])
        ckv = x @ Wkva
        compressed_kv, k_pe = (ckv[..., :KV_LORA], ckv[..., KV_LORA:])
        k_pe = jnp.broadcast_to(k_pe[:, :, None, :], (b, n, h, ROPE_DIM))
        kv = (compressed_kv @ Wkvb).reshape(b, n, h, NOPE_DIM + V_DIM)
        k_nope, v = (kv[..., :NOPE_DIM], kv[..., NOPE_DIM:])
        q_pe = rope(q_pe)
        k_pe = rope(k_pe)
        qf = jnp.concatenate([q_nope, q_pe], axis=-1)
        kf = jnp.concatenate([k_nope, k_pe], axis=-1)
        vf = jnp.pad(v, ((0, 0), (0, 0), (0, 0), (0, Q_HEAD_DIM - V_DIM)))
        scale = 1.0 / jnp.sqrt(jnp.asarray(Q_HEAD_DIM, dtype=qf.dtype))
        scores = jnp.einsum('bnhd,bmhd->bhnm', qf, kf) * scale
        mask = jnp.tril(jnp.ones((n, n), dtype=bool))
        scores = jnp.where(mask[None, None], scores, jnp.finfo(scores.dtype).min)
        probs = jax.nn.softmax(scores, axis=-1)
        out = jnp.einsum('bhnm,bmhd->bnhd', probs, vf)
        out = out[..., :V_DIM].reshape(b, n, h * V_DIM)
        return out @ Wo

    def _L0_ffn_ref(hidden_states, router_w, e_bias, W_gate, W_up, W_down, shared_gate, shared_up, shared_down):
        import math
        import jax, jax.numpy as jnp
        import numpy as np
        from jax import lax
        D = 512
        I = 256
        E = 32
        K = 4
        NG = 8
        TKG = 3
        NSH = 2
        SCALE = 2.5
        CF = 1.25
        B, S = (2, 512)

        def _router(x, router_w, e_bias):
            scores = jax.nn.sigmoid(x @ router_w.T)
            sc = scores + e_bias[None, :]
            T = x.shape[0]
            gs = sc.reshape(T, NG, E // NG)
            group_scores = lax.top_k(gs, 2)[0].sum(-1)
            _, gidx = lax.top_k(group_scores, TKG)
            gmask = jnp.zeros((T, NG), sc.dtype).at[jnp.arange(T)[:, None], gidx].set(1.0)
            smask = jnp.repeat(gmask, E // NG, axis=1)
            masked = jnp.where(smask > 0, sc, 0.0)
            _, topk_idx = lax.top_k(masked, K)
            topk_w = jnp.take_along_axis(scores, topk_idx, axis=1)
            topk_w = topk_w / (topk_w.sum(-1, keepdims=True) + 1e-20)
            topk_w = topk_w * SCALE
            return (topk_idx.astype(jnp.int32), topk_w)

        def _moe_forward(hidden_states, router_w, e_bias, W_gate, W_up, W_down, shared_gate, shared_up, shared_down):
            b, s, d = hidden_states.shape
            T = b * s
            C = int(math.ceil(CF * T / E))
            EC = E * C
            x = hidden_states.reshape(T, d)
            topk_idx, topk_w = _router(x, router_w, e_bias)
            expert_flat = topk_idx.reshape(-1)
            w_flat = topk_w.reshape(-1)
            tok_flat = jnp.repeat(jnp.arange(T, dtype=jnp.int32), K)
            sort_ix = jnp.argsort(expert_flat)
            e_sorted = expert_flat[sort_ix]
            tok_s = tok_flat[sort_ix]
            w_s = w_flat[sort_ix]
            counts = jnp.zeros(E, jnp.int32).at[e_sorted].add(1)
            group_start = jnp.concatenate([jnp.zeros(1, jnp.int32), jnp.cumsum(counts)[:-1].astype(jnp.int32)])
            pos = jnp.arange(T * K, dtype=jnp.int32) - group_start[e_sorted]
            valid = pos < C
            dest = e_sorted * C + jnp.where(valid, pos, 0)
            slots_token = jnp.zeros(EC, jnp.int32).at[dest].add(jnp.where(valid, tok_s, 0))
            slots_w = jnp.zeros(EC, w_s.dtype).at[dest].add(jnp.where(valid, w_s, 0.0))
            Xp = x[slots_token].reshape(E, C, d)
            G = jnp.einsum('ecd,edi->eci', Xp, W_gate)
            U = jnp.einsum('ecd,edi->eci', Xp, W_up)
            Y = jnp.einsum('eci,eid->ecd', jax.nn.silu(G) * U, W_down)
            Yf = Y.reshape(EC, d) * slots_w[:, None]
            out = jnp.zeros((T, d), x.dtype).at[slots_token].add(Yf)
            shared = jax.nn.silu(x @ shared_gate.T) * (x @ shared_up.T) @ shared_down.T
            return (out + shared).reshape(b, s, d)
        return _moe_forward(hidden_states, router_w, e_bias, W_gate, W_up, W_down, shared_gate, shared_up, shared_down)
    x = x + _L0_xattn_ref(_layernorm(x, axis=-1), ctx_512, L0_xattn_Wq, L0_xattn_w_kc_q, L0_xattn_w_kc_kv, L0_xattn_W_qr, L0_xattn_W_kr, L0_xattn_Wo)
    x = x + _L0_attn_ref(_layernorm(x, axis=-1), L0_attn_Wqa, L0_attn_Wqb, L0_attn_Wkva, L0_attn_Wkvb, L0_attn_Wo)
    x = x + _L0_ffn_ref(_layernorm(x, axis=-1), L0_ffn_router_w, L0_ffn_e_bias, L0_ffn_W_gate, L0_ffn_W_up, L0_ffn_W_down, L0_ffn_shared_gate, L0_ffn_shared_up, L0_ffn_shared_down)
    return x

_drawn_inputs = setup_inputs


def setup_inputs(seed=0):
    import zlib

    import numpy as np

    out = dict(_drawn_inputs(seed))
    spreads = {'L0_ffn_e_bias': (0.0, 0.501)}
    factors = {'L0_attn_Wqa': 8.0,
     'L0_attn_Wqb': 8.0,
     'L0_attn_Wkva': 3.142,
     'L0_attn_Wkvb': 2.816,
     'L0_attn_Wo': 2.767,
     'L0_ffn_router_w': 4.112,
     'L0_ffn_W_gate': 3.872,
     'L0_ffn_W_up': 3.867,
     'L0_ffn_W_down': 3.859}
    for name, (base, spread) in spreads.items():
        noise = np.random.default_rng([zlib.crc32(name.encode()), seed]).standard_normal(out[name].shape)
        drawn = base * np.exp(spread * noise) if base else spread * noise
        out[name] = jnp.asarray(drawn.astype(out[name].dtype))
    for name, factor in factors.items():
        out[name] = (out[name] * factor).astype(out[name].dtype)
    return out
```

```python
from contextlib import ExitStack

import numpy as np

import concourse.bass as bass
from concourse import mybir

F32 = mybir.dt.float32
BF16 = mybir.dt.bfloat16
ACT = mybir.ActivationFunctionType
ALU = mybir.AluOpType
AX = mybir.AxisListType

P = 128
T = 256
TT = T // P
D = 512
DC = D // P
L = 4096
LT = L // P
H = 16
NPAIR = H // 2
K = 128
CQ = 384
R = 64
GROUP = 4
SLOTS = 2 * LT // GROUP
HALF = SLOTS // 2
VW = 2 * K + 1
NH2 = 16
PE2, NOPE = 64, 32
QW = PE2 + NOPE
V2 = 32
E = 32
FI = 256
FC = FI // P
CAP = 10
SLOT = 32
GE = P // SLOT
NG = E // GE
W_GU = DC * 2 * FI
W_EXP = W_GU + FC * D
RING = 8
ROUTE_GROUPS, TOP_GROUPS, TOP_EXPERTS, ROUTE_SCALE = 8, 3, 4, 2.5
NEG = -3.0e38
EPS = 1e-5

C_ID, C_MASK, C_EARLY, C_ONES, C_IOTA, C_COS, C_SIN = 0, 128, 512, 640, 768, 784, 1040
C_END = 1296
W_PAIR = DC * 2 * K + (CQ // P) * 2 * K + (CQ // P) * 2 * R


def aux_plan():
    keys = [("k", c) for c in range(8)]
    maxima = [("m", c, j, st) for c in range(8) for j in range(2) for st in range(TT)]
    plan = [[] for _ in range(SLOTS)]
    for s in range(1, 5):
        plan[s] = [keys.pop(0), keys.pop(0), maxima.pop(0)]
    for s in range(5, 14):
        plan[s] = [maxima.pop(0) for _ in range(3)]
    plan[14] = maxima + [("t", 0), ("t", 1)]
    n = 0
    for s in range(SLOTS):
        for i, step in enumerate(plan[s]):
            plan[s][i] = (n, step)
            n += 1
    return plan, n


PLAN, AUX = aux_plan()
LAST_KEY = max(n for s in PLAN for n, step in s if step[0] == "k")
LAST_MAX = max(n for s in PLAN for n, step in s if step[0] == "m")


def before_loop():
    pieces = []
    for h in range(H + 1):
        if h < H:
            pieces += [("hk", h, c) for c in range(DC)] + [("b", h)]
        if h:
            pieces.append(("e", h - 1))
    steps = [("x", n, step) for slot in PLAN for n, step in slot]
    order, pieces = pieces[:ROPE_AFTER], pieces[ROPE_AFTER:]
    for n in range(4):
        order += [("rope", n)] + pieces[:PER_ROPE]
        pieces = pieces[PER_ROPE:]
    while pieces:
        order.append(pieces.pop(0))
        if len(steps) > 2:
            order.append(steps.pop(0))
    return order + steps


ROPE_AFTER, PER_ROPE = 18, 8
BEFORE = before_loop()
PAIR_BUFS = 6


def wait(eng, sem, value):
    if isinstance(value, int) and value <= 0:
        return
    eng.wait_ge(sem, value)


def wait_apart(eng, sem, value, passed):
    if not isinstance(value, int):
        eng.wait_ge(sem, value)
        eng.sem_inc(passed, 1)
    else:
        wait(eng, sem, value)


def layer(nc, a, out, stage=3):
    with ExitStack() as ctx:
        def sb(name, shape, dt=F32):
            return ctx.enter_context(nc.sbuf_tensor(name, shape, dt))

        def ps(name, cols):
            return ctx.enter_context(nc.psum_tensor(name, [P, cols], F32))

        def sem(name):
            return ctx.enter_context(nc.semaphore(name))

        top = [0]
        arena = sb("arena", [P, 53100])

        def cut(cols, at=None):
            o = top[0] if at is None else at
            if at is None:
                top[0] += cols
            return arena[:, o:o + cols]

        vx = cut(LT * VW // 2).bitcast(BF16).rearrange("p (t w) -> p t w", w=VW)
        kt_hi = cut(L // 2).bitcast(BF16)
        kt_lo = cut(L // 2).bitcast(BF16)
        stage_at = top[0]
        k_hi = cut(L // 2).bitcast(BF16)
        k_lo = cut(L // 2).bitcast(BF16)
        k1_at = top[0]
        k1 = cut(L).bitcast(BF16).rearrange("p (j l) -> p j l", j=2)
        k2_at = top[0]
        k2 = cut(L).bitcast(BF16).rearrange("p (j l) -> p j l", j=2)
        p_f = cut(2048).rearrange("p (b n) -> p b n", b=2)
        p_hi = cut(1024).bitcast(BF16).rearrange("p (b n) -> p b n", b=2)
        p_lo = cut(1024).bitcast(BF16).rearrange("p (b n) -> p b n", b=2)
        q_at = top[0]
        q1_all = cut(H * T // 2).bitcast(BF16).rearrange("p (h s) -> p h s", h=H)
        q2_all = cut(H * T // 2).bitcast(BF16).rearrange("p (h s) -> p h s", h=H)
        r_at = top[0]
        wkv = cut(H * K).rearrange("p (h k) -> p h k", h=H)
        wo1 = cut(H * D).rearrange("p (h n) -> p h n", h=H)
        ctx_all = cut(TT * H * K).rearrange("p (s h d) -> p s h d", s=TT, h=H)
        x = cut(TT * D).rearrange("p (s d) -> p s d", s=TT)
        xn = cut(TT * D).rearrange("p (s d) -> p s d", s=TT)
        xnT = cut(DC * T).rearrange("p (c s) -> p c s", c=DC)
        const = cut(C_END)
        w_at = top[0]
        wkr_hi = cut(512).bitcast(BF16)
        wkr_lo = cut(512).bitcast(BF16)
        wkr_now = cut(128).bitcast(BF16).rearrange("p (b n) -> p b n", b=2)
        q_max = cut(256).bitcast(BF16).rearrange("p (j s) -> p j s", j=2)
        q1 = cut(256).bitcast(BF16).rearrange("p (j s) -> p j s", j=2)
        q2 = cut(256).bitcast(BF16).rearrange("p (j s) -> p j s", j=2)
        ident_b = cut(64).bitcast(BF16)
        bn = cut(16)
        mv = cut(8)
        maxes = cut(32).rearrange("p (j s c) -> p (j s) c", j=2, s=TT)
        mx4 = cut(4)
        negm = cut(2).bitcast(BF16)
        rsum = cut(4)
        ctx_in = arena[:, k1_at:k1_at + L].rearrange("p (t d) -> p t d", t=LT)
        rope = arena[:, k2_at:k2_at + L].rearrange("p (t c i) -> p t c i", t=LT, c=2)
        kr = arena[:, stage_at:stage_at + 2048].rearrange("p (b t d) -> p b t d", b=2, t=8)
        kr2 = arena[:, stage_at + 2048:stage_at + 4096].rearrange("p (b t d) -> p b t d", b=2, t=8)
        w_pair = arena[:, r_at:r_at + PAIR_BUFS * W_PAIR].rearrange("p (b n) -> p b n", b=PAIR_BUFS)
        wkr_in = arena[:, r_at + PAIR_BUFS * W_PAIR:r_at + PAIR_BUFS * W_PAIR + H * R]
        b_dup = arena[:, r_at + 14080:r_at + 14336].rearrange("p (b n) -> p b n", b=2)
        ctxT = arena[:, q_at + 3072:q_at + 3584].rearrange("p (b n) -> p b n", b=2)
        latT = arena[:, q_at + 3584:q_at + 4096].rearrange("p (b n) -> p b n", b=2)

        w_qb = arena[:, q_at:q_at + 2048].rearrange("p (h w) -> p h w", h=NH2)
        w_kvb = arena[:, q_at + 2048:q_at + 3072]
        w_kb = w_kvb[:, 0:512].rearrange("p (h w) -> p h w", h=NH2)
        w_vb = w_kvb[:, 512:1024]
        qa = arena[:, q_at + 3072:q_at + 3328]
        ckv = arena[:, q_at + 3328:q_at + 3584]
        rope_b = arena[:, q_at + 3584:q_at + 4096].rearrange("p (b n) -> p b n", b=2)
        w_a = cut(DC * (P + P + 3 * V2))
        w_qa = w_a[:, 0:512].rearrange("p (c n) -> p c n", c=DC)
        w_kva = w_a[:, 512:1024].rearrange("p (c n) -> p c n", c=DC)
        w_kpe = w_a[:, 1024:1408].rearrange("p (c n) -> p c n", c=DC)
        qhk = arena[:, top[0]:top[0] + 2 * T].rearrange("p (b n) -> p b n", b=2)
        wo2 = cut(DC * D).rearrange("p (c n) -> p c n", c=DC)
        qf = arena[:, r_at:r_at + 4096].rearrange("p (h n) -> p h n", h=NH2)
        kf = arena[:, r_at + 4096:r_at + 8192].rearrange("p (h n) -> p h n", h=NH2)
        sm = arena[:, r_at + 8192:r_at + 14336].rearrange("p (h n) -> p h n", h=NH2)
        pT = arena[:, w_at:w_at + 768].rearrange("p (b n) -> p b n", b=2)
        v2 = arena[:, w_at + 768:w_at + 1792].rearrange("p (s n) -> p s n", s=TT)
        negm2 = arena[:, w_at + 1792:w_at + 1824].rearrange("p (h s) -> p h s", h=NH2)
        sums2 = arena[:, w_at + 1824:w_at + 1856].rearrange("p (s h) -> p s h", h=NH2)
        rsum2 = arena[:, w_at + 1856:w_at + 1888].rearrange("p (s h) -> p s h", h=NH2)

        ring = arena[:, 0:RING * W_EXP].rearrange("p (e n) -> p e n", e=RING)
        w_router = cut(DC * E).rearrange("p (c e) -> p c e", c=DC)
        bias_e = cut(E)
        sg = arena[:, r_at:r_at + 2048].rearrange("p (c n) -> p c n", c=DC)
        su = arena[:, r_at + 2048:r_at + 4096].rearrange("p (c n) -> p c n", c=DC)
        sd = arena[:, r_at + 4096:r_at + 6144].rearrange("p (c n) -> p c n", c=DC)
        xpT = arena[:, r_at + 6144:r_at + 10240].rearrange("p (c e s) -> p c e s", c=DC, e=E)
        owT = arena[:, r_at + 10240:r_at + 12288].rearrange("p (g t) -> p g t", g=NG)
        hs = arena[:, r_at + 12288:r_at + 13312].rearrange("p (c t) -> p c t", c=DC)
        y = arena[:, r_at + 13312:r_at + 14336].rearrange("p (b n) -> p b n", b=2)
        oh = arena[:, q_at:q_at + 2048].rearrange("p (t e s) -> p t e s", t=TT, e=E)
        ow = arena[:, q_at + 2048:q_at + 4096].rearrange("p (t e s) -> p t e s", t=TT, e=E)
        hid = arena[:, w_at:w_at + 512].rearrange("p (b n) -> p b n", b=2)
        hT = arena[:, w_at + 512:w_at + 1024].rearrange("p (b c n) -> p b c n", b=2, c=FC)
        small = [arena[:, w_at + 1024 + 64 * i:w_at + 1088 + 64 * i] for i in range(14)]

        ident = const[:, C_ID:C_ID + P]

        psS = [ps(f"psS{i}", 1024) for i in range(2)]
        psO = [ps(f"psO{i}", 512) for i in range(2)]
        psA = [ps(f"psA{i}", 512) for i in range(2)]
        psE = [psS[0][:, 0:512], psS[0][:, 512:1024]]
        psF = [psS[1][:, 0:512], psS[1][:, 512:1024]]

        ld_x, ld_const, ld_ctx, ld_rope, ld_wkr = (sem(n) for n in ("ld_x", "ld_const", "ld_ctx", "ld_rope", "ld_wkr"))
        ld_pair = [sem(f"ld_pair{i}") for i in range(PAIR_BUFS)]
        ld_wkv, ld_wo1 = sem("ld_wkv"), sem("ld_wo1")
        dve_step, act_step = sem("dve_step"), sem("act_step")
        ident_done = sem("ident_done")
        ln_var, ln_std, ln_xn, ln_tr, ln_T = (sem(n) for n in ("ln_var", "ln_std", "ln_xn", "ln_tr", "ln_T"))
        rot_done, kr_done, vhi_done, vlo_done, krT_done, kthi_done, ktlo_done = (
            sem(n) for n in ("rot_done", "kr_done", "vhi_done", "vlo_done", "krT_done", "kthi_done", "ktlo_done"))
        ones_done, wkr_split = sem("ones_done"), sem("wkr_split")
        b_mm, b_copied, qhk_mm, qhk_copied, q_mm, qhi_done, qlo_done = (
            sem(n) for n in ("b_mm", "b_copied", "qhk_mm", "qhk_copied", "q_mm", "qhi_done", "qlo_done"))
        s_scores, s_phi, s_pf, s_plo, s_pv, s_out = (
            sem(n) for n in ("s_scores", "s_phi", "s_pf", "s_plo", "s_pv", "s_out"))
        s_aux, s_khi, s_free, s_negm, s_mx, s_out1 = (sem(n) for n in ("s_aux", "s_khi", "s_free", "s_negm", "s_mx", "s_out1"))
        k_copied = [sem(f"k_copied{j}") for j in range(2)]
        qmax_copied = sem("qmax_copied")
        ct_mm, ct_copied, lat_mm, lat_copied, o1_mm, x1_done = (
            sem(n) for n in ("ct_mm", "ct_copied", "lat_mm", "lat_copied", "o1_mm", "x1_done"))
        stored = sem("stored")
        ld_wa, ld_wo2, ld_qb, ld_kvb, ld_router, ld_bias = (
            sem(n) for n in ("ld_wa", "ld_wo2", "ld_qb", "ld_kvb", "ld_router", "ld_bias"))
        qa_mm, qa_copied, kpe_mm, kpe_done, kpe_spread, kn_mm, kn_copied, v_mm, v_copied = (
            sem(n) for n in ("qa_mm", "qa_copied", "kpe_mm", "kpe_done", "kpe_spread", "kn_mm", "kn_copied", "v_mm", "v_copied"))
        q2_mm, q2_done, s2_mm, s2_max, s2_exp, pT_mm, pT_copied, o2_mm, o2_done, o2T_mm, o2T_copied, x2_mm, x2_done = (
            sem(n) for n in ("q2_mm", "q2_done", "s2_mm", "s2_max", "s2_exp", "pT_mm", "pT_copied", "o2_mm", "o2_done",
                             "o2T_mm", "o2T_copied", "x2_mm", "x2_done"))
        ld_shared = [sem(f"ld_shared{i}") for i in range(3)]
        ld_gu = [sem(f"ld_gu{i}") for i in range(RING)]
        ld_down = [sem(f"ld_down{i}") for i in range(RING)]
        cleared, logit_mm, sig_exp, sel_done, pos_mm, oh_done, ow_done, xp_mm, xp_copied, owT_mm, owT_copied = (
            sem(n) for n in ("cleared", "logit_mm", "sig_exp", "sel_done", "pos_mm", "oh_done", "ow_done", "xp_mm",
                             "xp_copied", "owT_mm", "owT_copied"))
        sh_mm, sh_silu, sh_done, gu_mm, gu_silu, hid_done, hT_mm, hT_copied, y_mm, y_copied, comb_mm, x3_done = (
            sem(n) for n in ("sh_mm", "sh_silu", "sh_done", "gu_mm", "gu_silu", "hid_done", "hT_mm", "hT_copied",
                             "y_mm", "y_copied", "comb_mm", "x3_done"))
        sp_passed, pool_passed = sem("sp_passed"), sem("pool_passed")

        block = ctx.enter_context(nc.Block())

        @block.sync
        def _(sp):
            sp.dma_start(x, a["x"].rearrange("a (s p) d -> p (a s) d", p=P)).then_inc(ld_x, 16)
            sp.dma_start(const, a["const"]).then_inc(ld_const, 16)
            for n in range(2):
                sp.dma_start(w_pair[:, n, :], a["w_pair"][n]).then_inc(ld_pair[n], 16)
            sp.dma_start(ctx_in, a["ctx"]).then_inc(ld_ctx, 16)
            sp.dma_start(rope, a["rope"]).then_inc(ld_rope, 16)
            for n in range(2, NPAIR):
                if n >= PAIR_BUFS:
                    sp.wait_ge(b_mm, 2 * (n - PAIR_BUFS + 1))
                sp.dma_start(w_pair[:, n % PAIR_BUFS, :], a["w_pair"][n]).then_inc(ld_pair[n % PAIR_BUFS], 16)
                if n == 2:
                    sp.dma_start(wkr_in, a["w_kr"]).then_inc(ld_wkr, 16)

            def copy_keys(q):
                for j in range(2):
                    src = slice(R * j, R * j + R)
                    wait_apart(sp, s_free, q * AUX + LAST_KEY + 1, sp_passed)
                    wait_apart(sp, s_scores, (q - 1) * SLOTS + HALF * (j + 1), sp_passed)
                    sp.dma_start(k1[0:R, j, :], k_hi[src, :]).then_inc(k_copied[j], 16)
                    sp.dma_start(k1[R:2 * R, j, :], k_lo[src, :]).then_inc(k_copied[j], 16)
                    sp.dma_start(k2[0:R, j, :], k_hi[src, :]).then_inc(k_copied[j], 16)
                    sp.dma_start(q1[:, j, :], q1_all[:, bass.ds(q * 2 + j, 1), :].rearrange("p a s -> p (a s)")).then_inc(k_copied[j], 16)
                    sp.dma_start(q2[0:R, j, :], q2_all[0:R, bass.ds(q * 2 + j, 1), :].rearrange("p a s -> p (a s)")).then_inc(k_copied[j], 16)
            sp.wait_ge(qhi_done, 2)
            sp.wait_ge(qlo_done, 2)
            copy_keys(0)
            sp.wait_ge(qhi_done, H)
            sp.wait_ge(qlo_done, H)
            sp.dma_start(w_a, a["w_a"]).then_inc(ld_wa, 16)
            sp.dma_start(wo2, a["w_o2"]).then_inc(ld_wo2, 16)
            sp.dma_start(w_router, a["w_router"]).then_inc(ld_router, 16)
            sp.dma_start(bias_e, a["e_bias"].partition_broadcast(P)).then_inc(ld_bias, 16)
            sp.dma_start(wkv, a["w_kv"]).then_inc(ld_wkv, 16)
            sp.dma_start(wo1, a["w_o1"]).then_inc(ld_wo1, 16)
            with sp.Fori(1, NPAIR) as q:
                copy_keys(q)
            sp.wait_ge(s_pv, NPAIR * SLOTS)
            sp.dma_start(w_qb, a["w_qb"]).then_inc(ld_qb, 16)
            sp.dma_start(w_kvb, a["w_kvb"]).then_inc(ld_kvb, 16)
            for e in range(RING):
                sp.dma_start(ring[:, e, 0:W_GU], a["w_exp"][e][:, 0:W_GU]).then_inc(ld_gu[e], 16)
                sp.dma_start(ring[:, e, W_GU:W_EXP], a["w_exp"][e][:, W_GU:W_EXP]).then_inc(ld_down[e], 16)
            sp.wait_ge(s2_mm, NH2)
            for i, w in enumerate((sg, su, sd)):
                sp.dma_start(w, a["w_shared"][i]).then_inc(ld_shared[i], 16)
            for e in range(RING, E):
                sp.wait_ge(gu_mm, (e - RING) // GE + 1)
                sp.dma_start(ring[:, e % RING, 0:W_GU], a["w_exp"][e][:, 0:W_GU]).then_inc(ld_gu[e % RING], 16)
                if e % GE == GE - 1:
                    sp.wait_ge(y_mm, (e - RING) // GE + 1)
                    for d in range(e - GE + 1, e + 1):
                        sp.dma_start(ring[:, d % RING, W_GU:W_EXP], a["w_exp"][d][:, W_GU:W_EXP]).then_inc(ld_down[d % RING], 16)
            sp.wait_ge(x3_done, 1)
            sp.dma_start(out.rearrange("a (s p) d -> p (a s) d", p=P), x).then_inc(stored, 16)
            sp.wait_ge(stored, 16)

        @block.gpsimd
        def _(pool):
            for n in range(4):
                if n == 0:
                    pool.wait_ge(ld_ctx, 16)
                    pool.wait_ge(ld_rope, 16)
                wait(pool, kr_done, n - 1)
                t = slice(8 * n, 8 * n + 8)
                for half in range(2):
                    sin = rope[:, t, 1, 32 * half:32 * half + 32].unsqueeze(3).to_broadcast([P, 8, 32, 2])
                    o = slice(64 * half, 64 * half + 64)
                    i = slice(64 - 64 * half, 128 - 64 * half)
                    nc.gpsimd.tensor_tensor(kr2[:, n % 2, :, o].rearrange("p t (i e) -> p t i e", e=2),
                                            ctx_in[:, t, i].rearrange("p t (i e) -> p t i e", e=2),
                                            sin, ALU.mult).then_inc(rot_done, 1)

            def bring(q):
                wait_apart(pool, s_aux, (q - 1) * AUX + LAST_MAX + 1, pool_passed)
                h = q * 2
                nc.gpsimd.tensor_copy(q_max, q1_all[:, bass.ds(h, 2), :]).then_inc(qmax_copied, 1)
                nc.gpsimd.tensor_copy(wkr_now[:, 0, :], wkr_hi[:, bass.ds(q * P, P)]).then_inc(qmax_copied, 1)
                nc.gpsimd.tensor_copy(wkr_now[:, 1, :], wkr_lo[:, bass.ds(q * P, P)]).then_inc(qmax_copied, 1)
            pool.wait_ge(qhi_done, 2)
            pool.wait_ge(wkr_split, 2)
            bring(0)
            pool.wait_ge(kr_done, 4)
            pool.wait_ge(qmax_copied, 3)
            one2 = float(np.array([0x3F803F80], np.uint32).view(np.float32)[0])
            nc.gpsimd.memset(arena[R:R + 1, k2_at:k2_at + L], one2).then_inc(ones_done, 1)
            pool.wait_ge(ones_done, 1)
            pool.wait_ge(qhi_done, H)
            with pool.Fori(1, NPAIR) as q:
                bring(q)
            pool.wait_ge(x2_mm, 1)
            nc.gpsimd.memset(arena[:, q_at:q_at + 4096], 0.0).then_inc(cleared, 1)
            nc.gpsimd.memset(arena[:, r_at + 6144:r_at + 10240], 0.0).then_inc(cleared, 1)

        @block.scalar
        def _(act):
            def std(n):
                act.wait_ge(ln_var, n)
                nc.scalar.activation(mv.rearrange("p (s c) -> p s c", c=4)[:, 0:TT, 2], mv.rearrange("p (s c) -> p s c", c=4)[:, 0:TT, 1], ACT.Sqrt).then_inc(ln_std, 1)
                act.wait_ge(ln_tr, n)
                nc.scalar.copy(xnT.rearrange("p c s -> p (c s)"), psS[0][:, :]).then_inc(ln_T, 1)
            std(1)
            def rope_high(n):
                act.wait_ge(kr_done, n + 1)
                nc.scalar.copy(vx[:, 8 * n:8 * n + 8, 0:K], kr[:, n % 2]).then_inc(vhi_done, 1)
                act.wait_ge(krT_done, n + 1)
                nc.scalar.copy(kt_hi[:, 1024 * n:1024 * n + 1024], psS[0][:, :]).then_inc(kthi_done, 1)
                if n == 0:
                    act.wait_ge(ld_wkr, 16)
                    nc.scalar.copy(wkr_hi, wkr_in).then_inc(wkr_split, 1)

            def query(what, h):
                if what == "hk":
                    act.wait_ge(qhk_mm, h + 1)
                    wait(act, q_mm, h - 1)
                    nc.scalar.copy(qhk[:, h % 2, :], psO[h % 2][:, 0:T]).then_inc(qhk_copied, 1)
                elif what == "b":
                    act.wait_ge(b_mm, h + 1)
                    nc.scalar.copy(b_dup[:, h % 2, :].rearrange("p (a r) -> p a r", a=2),
                                   psF[h % 2][:, 0:R].unsqueeze(1).to_broadcast([P, 2, R])).then_inc(b_copied, 1)
                else:
                    act.wait_ge(q_mm, h + 1)
                    nc.scalar.copy(q1_all[:, h, :], psF[h % 2][:, T:2 * T]).then_inc(qhi_done, 1)

            def aux(q, n, step):
                if step[0] == "k":
                    act.wait_ge(s_aux, q * AUX + n + 1)
                    wait(act, k_copied[0], q * 80)
                    wait(act, k_copied[1], q * 80)
                    nc.scalar.copy(k_hi[:, 512 * step[1]:512 * step[1] + 512], psA[n % 2][:, :]).then_inc(s_khi, 1)

            def body(p, ahead=True):
                for s in range(SLOTS):
                    t = p * SLOTS + s
                    act.wait_ge(s_scores, t + 1)
                    wait(act, s_pv, t - 1)
                    nc.scalar.activation(p_hi[:, s % 2, :], psS[s % 2][:, :], ACT.Exp).then_inc(s_phi, 1)
                    wait(act, s_plo, t - 1)
                    nc.scalar.activation(p_f[:, s % 2, :], psS[s % 2][:, :], ACT.Exp).then_inc(s_pf, 1)
                    if ahead:
                        for n, step in PLAN[s]:
                            aux(p + 1, n, step)
            for what, n, *rest in BEFORE:
                if what == "rope":
                    rope_high(n)
                elif what == "x":
                    aux(0, n, *rest)
                elif what != "hk" or rest[0] == DC - 1:
                    query(what, n)
            body(0)
            with act.Fori(1, NPAIR - 1) as p:
                body(p)
            body(NPAIR - 1, ahead=False)
            for h in range(H):
                act.wait_ge(ct_mm, h + 1)
                wait(act, lat_mm, h - 1)
                nc.scalar.copy(ctxT[:, h % 2, :], psS[0][:, 512 * (h % 2):512 * (h % 2) + T]).then_inc(ct_copied, 1)
            std(2)
            act.wait_ge(qa_mm, 1)
            nc.scalar.copy(qa, psA[0][:, 0:T]).then_inc(qa_copied, 1)
            act.wait_ge(qa_mm, 2)
            nc.scalar.copy(ckv, psA[1][:, 0:T]).then_inc(qa_copied, 1)
            act.wait_ge(kpe_done, 1)
            nc.scalar.copy(kf[0:PE2, 1:NH2, :], kf[0:PE2, 0:1, :].to_broadcast([PE2, NH2 - 1, T])).then_inc(kpe_spread, 1)
            for n in range(NH2 // 2):
                act.wait_ge(kn_mm, n + 1)
                nc.scalar.copy(kf[PE2:QW, 2 * n:2 * n + 2, :].rearrange("p h n -> p (h n)"), psA[n % 2][PE2:QW, :]).then_inc(kn_copied, 1)

            def exps(h):
                act.wait_ge(s2_max, h + 1)
                nc.scalar.activation(sm[:, h, 0:P], sm[:, h, 0:P], ACT.Exp, bias=negm2[:, h, 0:1],
                                     accum_out=sums2[:, 0, h:h + 1]).then_inc(s2_exp, 1)
                nc.scalar.activation(sm[:, h, P:3 * P], sm[:, h, P:3 * P], ACT.Exp, bias=negm2[:, h, 1:2],
                                     accum_out=sums2[:, 1, h:h + 1]).then_inc(s2_exp, 1)
            for h in range(NH2 + 1):
                if h < NH2:
                    exps(h)
                if h:
                    act.wait_ge(pT_mm, h)
                    wait(act, o2_mm, h - 2)
                    nc.scalar.copy(pT[:, (h - 1) % 2, :], psA[(h - 1) % 2][:, 0:3 * P]).then_inc(pT_copied, 1)
            act.wait_ge(o2T_mm, 1)
            nc.scalar.copy(xnT.rearrange("p c s -> p (c s)"), psS[0][:, :]).then_inc(o2T_copied, 1)
            std(3)
            act.wait_ge(logit_mm, 1)
            nc.scalar.activation(small[0], psA[0][:, 0:TT * E], ACT.Exp, scale=-1.0).then_inc(sig_exp, 1)
            for i in range(DC):
                act.wait_ge(sh_mm, i + 1)
                nc.scalar.activation(hs[:, i, :], psF[i % 2][:, 0:T], ACT.Silu).then_inc(sh_silu, 1)
            for c in range(DC):
                act.wait_ge(xp_mm, c + 1)
                nc.scalar.copy(xpT[:, c, :, 0:CAP], psE[c % 2][:, 0:E * CAP].rearrange("p (e s) -> p e s", e=E)).then_inc(xp_copied, 1)
            for i in range(NG // 2):
                act.wait_ge(owT_mm, i + 1)
                nc.scalar.copy(owT[:, 2 * i:2 * i + 2, :].rearrange("p g t -> p (g t)"), psA[i % 2][:, :]).then_inc(owT_copied, 1)
            for g in range(NG):
                act.wait_ge(gu_mm, g + 1)
                wait(act, hT_mm, g - 1)
                nc.scalar.activation(hid[:, g % 2, :], psF[g % 2][:, 0:FI], ACT.Silu).then_inc(gu_silu, 1)
                act.wait_ge(hT_mm, g + 1)
                wait(act, y_mm, g - 1)
                nc.scalar.copy(hT[:, g % 2].rearrange("p c n -> p (c n)"), psE[g % 2][:, 0:FI]).then_inc(hT_copied, 1)

        @block.vector
        def _(dve):
            def low_query(h):
                dve.wait_ge(qhi_done, h + 1)
                nc.vector.tensor_tensor(q2_all[0:R, h, :], psF[h % 2][0:R, T:2 * T], q1_all[0:R, h, :], ALU.subtract).then_inc(qlo_done, 1)

            steps = [0]

            def link(ins):
                steps[0] += 1
                ins.then_inc(dve_step, 1)
                dve.wait_ge(dve_step, steps[0])

            def layernorm(n):
                st = bn[:, 0:12].rearrange("p (s c) -> p s c", c=6)
                m = mv.rearrange("p (s c) -> p s c", c=4)
                for s in range(TT):
                    link(nc.vector.bn_stats(st[:, s, :], x[:, s, :]))
                for s in range(TT):
                    link(nc.vector.bn_aggr(m[:, s, 0:2], st[:, s, :]))
                nc.vector.tensor_scalar_add(m[:, 0:TT, 1], m[:, 0:TT, 1], EPS).then_inc(ln_var, 1)
                dve.wait_ge(ln_std, n)
                link(nc.vector.reciprocal(m[:, 0:TT, 3], m[:, 0:TT, 2]))
                for s in range(TT):
                    nc.vector.tensor_scalar(xn[:, s, :], x[:, s, :], m[:, s, 0:1], m[:, s, 3:4],
                                            ALU.subtract, ALU.mult).then_inc(ln_xn, 1)
            dve.wait_ge(ld_const, 16)
            nc.vector.tensor_copy(ident_b, ident).then_inc(ident_done, 1)
            link(nc.vector.memset(vx[:, :, K:K + 1], 1.0))
            dve.wait_ge(ld_x, 16)
            layernorm(1)
            def rope_rows(n):
                t = slice(8 * n, 8 * n + 8)
                if n == 0:
                    dve.wait_ge(ld_ctx, 16)
                    dve.wait_ge(ld_rope, 16)
                wait(dve, vhi_done, n - 1)
                wait(dve, krT_done, n - 1)
                link(nc.vector.tensor_tensor(kr[:, n % 2].rearrange("p t (i e) -> p t i e", e=2),
                                             ctx_in[:, t, :].rearrange("p t (i e) -> p t i e", e=2),
                                             rope[:, t, 0, :].unsqueeze(3).to_broadcast([P, 8, 64, 2]), ALU.mult))
                dve.wait_ge(rot_done, 2 * n + 2)
                nc.vector.tensor_tensor(kr[:, n % 2], kr[:, n % 2], kr2[:, n % 2], ALU.add).then_inc(kr_done, 1)

            def rope_low(n):
                t = slice(8 * n, 8 * n + 8)
                dve.wait_ge(vhi_done, n + 1)
                nc.vector.tensor_tensor(vx[:, t, K + 1:VW], kr[:, n % 2], vx[:, t, 0:K], ALU.subtract).then_inc(vlo_done, 1)
                dve.wait_ge(vlo_done, n + 1)
                dve.wait_ge(kthi_done, n + 1)
                nc.vector.tensor_tensor(kt_lo[:, 1024 * n:1024 * n + 1024], psS[0][:, :],
                                        kt_hi[:, 1024 * n:1024 * n + 1024], ALU.subtract).then_inc(ktlo_done, 1)
                if n == 0:
                    dve.wait_ge(wkr_split, 1)
                    nc.vector.tensor_tensor(wkr_lo, wkr_in, wkr_hi, ALU.subtract).then_inc(wkr_split, 1)

            def aux(q, n, step):
                dve.wait_ge(s_aux, q * AUX + n + 1)
                if step[0] == "k":
                    c = slice(512 * step[1], 512 * step[1] + 512)
                    dve.wait_ge(s_khi, q * 8 + step[1] + 1)
                    nc.vector.tensor_tensor(k_lo[:, c], psA[n % 2][:, :], k_hi[:, c], ALU.subtract).then_inc(s_free, 1)
                elif step[0] == "m":
                    _, c, j, st = step
                    nc.vector.reduce_max(maxes[:, TT * j + st, c:c + 1], psA[n % 2][:, :], AX.X).then_inc(s_free, 1)
                else:
                    j = step[1]
                    nc.vector.tensor_copy(q2[R:R + 1, j, :], psA[n % 2][R:R + 1, 0:T]).then_inc(s_free, 1)
                if n == LAST_MAX:
                    dve.wait_ge(s_free, q * AUX + n + 1)
                    nc.vector.reduce_max(mx4, maxes, AX.X).then_inc(s_mx, 1)
                    dve.wait_ge(s_mx, q + 1)
                    nc.vector.tensor_scalar_mul(negm, mx4, -1.0).then_inc(s_negm, 1)

            def head_out(p, j):
                hd = p * 2 + j
                dve.wait_ge(s_pv, hd * HALF + HALF)
                for st in range(TT):
                    nc.vector.reciprocal(rsum[:, st:st + 1], psO[st][:, K:K + 1]).then_inc(s_out1, 1)
                for st in range(TT):
                    dve.wait_ge(s_out1, hd * 4 + 1 + st)
                    o = ctx_all[:, st, bass.ds(hd, 1), :].rearrange("p a d -> p (a d)")
                    nc.vector.tensor_scalar(o, psO[st][:, 0:K], rsum[:, st:st + 1], None, ALU.mult).then_inc(s_out1, 1)
                for st in range(TT):
                    dve.wait_ge(s_out1, hd * 4 + 3 + st)
                    o = ctx_all[:, st, bass.ds(hd, 1), :].rearrange("p a d -> p (a d)")
                    nc.vector.scalar_tensor_tensor(o, psO[st][:, K + 1:VW], rsum[:, st:st + 1], o, ALU.mult, ALU.add).then_inc(s_out, 1)

            def body(p, ahead=True):
                for s in range(SLOTS):
                    t = p * SLOTS + s
                    if s == HALF:
                        head_out(p, 0)
                    if s == 0 and not (isinstance(p, int) and p == 0):
                        head_out(p - 1, 1)
                    dve.wait_ge(s_pf, t + 1)
                    wait(dve, s_pv, t - 1)
                    nc.vector.tensor_tensor(p_lo[:, s % 2, :], p_f[:, s % 2, :], p_hi[:, s % 2, :], ALU.subtract).then_inc(s_plo, 1)
                    if ahead:
                        for n, step in PLAN[s]:
                            aux(p + 1, n, step)
            for what, n, *rest in BEFORE:
                if what == "e":
                    low_query(n)
                elif what == "rope":
                    if n == 0:
                        rope_rows(0)
                    if n < 3:
                        rope_rows(n + 1)
                    rope_low(n)
                elif what == "x":
                    aux(0, n, *rest)
            body(0)
            with dve.Fori(1, NPAIR - 1) as p:
                body(p)
            body(NPAIR - 1, ahead=False)
            head_out(NPAIR - 1, 1)
            for h in range(H):
                dve.wait_ge(lat_mm, h + 1)
                wait(dve, o1_mm, h - 1)
                nc.vector.tensor_copy(latT[:, h % 2, :], psA[h % 2][:, 0:T]).then_inc(lat_copied, 1)
            dve.wait_ge(o1_mm, H)
            for st in range(TT):
                ins = nc.vector.tensor_tensor(x[:, st, :], psO[st][:, :], x[:, st, :], ALU.add)
            ins.then_inc(x1_done, 1)
            dve.wait_ge(x1_done, 1)
            layernorm(2)
            cos2, sin2 = const[:, C_COS:C_COS + T], const[:, C_SIN:C_SIN + T]

            def roped(out_ap, bank, b, rows_a):
                link(nc.vector.tensor_tensor(out_ap[0:rows_a, :], bank[0:rows_a, 0:T], cos2[0:rows_a, :], ALU.mult))
                link(nc.vector.tensor_tensor(rope_b[0:PE2, b, :], bank[0:PE2, T:2 * T], sin2[0:PE2, :], ALU.mult))
                return nc.vector.tensor_tensor(out_ap[0:PE2, :], out_ap[0:PE2, :], rope_b[0:PE2, b, :], ALU.add)
            dve.wait_ge(kpe_mm, 1)
            roped(kf[:, 0, :], psO[0], 0, PE2).then_inc(kpe_done, 1)
            for st in range(TT):
                dve.wait_ge(v_mm, st + 1)
                nc.vector.tensor_copy(v2[:, st, :], psF[st]).then_inc(v_copied, 1)
            scale = float(np.float32(1.0) / np.sqrt(np.float32(QW)))
            for h in range(NH2 + 1):
                if h < NH2:
                    dve.wait_ge(q2_mm, h + 1)
                    roped(qf[:, h, :], psE[h % 2], h % 2, QW).then_inc(q2_done, 1)
                if h:
                    g = h - 1
                    dve.wait_ge(s2_mm, h)
                    link(nc.vector.scalar_tensor_tensor(sm[:, g, :], psF[g % 2][:, 0:3 * P], scale, const[:, C_MASK:C_MASK + 3 * P], ALU.mult, ALU.add))
                    nc.vector.tensor_reduce(negm2[:, g, 0:1], sm[:, g, 0:P], AX.X, ALU.max, negate=True)
                    nc.vector.tensor_reduce(negm2[:, g, 1:2], sm[:, g, P:3 * P], AX.X, ALU.max, negate=True).then_inc(s2_max, 1)
            dve.wait_ge(s2_exp, 2 * NH2)
            link(nc.vector.reciprocal(rsum2.rearrange("p s h -> p (s h)"), sums2.rearrange("p s h -> p (s h)")))
            dve.wait_ge(o2_mm, NH2)
            for st in range(TT):
                nc.vector.tensor_tensor(xn[:, st, :].rearrange("p (h v) -> p h v", h=NH2), psO[st][:, :].rearrange("p (h v) -> p h v", h=NH2),
                                        rsum2[:, st, :].unsqueeze(2).to_broadcast([P, NH2, V2]), ALU.mult).then_inc(o2_done, 1)
            dve.wait_ge(x2_mm, 1)
            for st in range(TT):
                ins = nc.vector.tensor_tensor(x[:, st, :], psA[st][:, :], x[:, st, :], ALU.add)
            ins.then_inc(x2_done, 1)
            dve.wait_ge(x2_done, 1)
            layernorm(3)

            def te(i):
                return small[i].rearrange("p (t e) -> p t e", t=TT)

            def first(out_ap, v, width, count, tmp):
                top8, gt, eq, cum, left = tmp
                n = slice(0, width)
                for t in range(TT):
                    link(nc.vector.max(top8[:, t, 0:8], v[:, t, n]))
                for t in range(TT):
                    thr = top8[:, t, count - 1:count]
                    link(nc.vector.tensor_scalar(gt[:, t, n], v[:, t, n], thr, None, ALU.is_gt))
                    link(nc.vector.tensor_scalar(eq[:, t, n], v[:, t, n], thr, None, ALU.is_equal))
                    link(nc.vector.tensor_tensor_scan(cum[:, t, n], ones_e[:, t, n], eq[:, t, n], 0.0, ALU.mult, ALU.add))
                link(nc.vector.reduce_sum(left[:, 0:TT, 0], gt[:, :, n], AX.X))
                link(nc.vector.tensor_scalar(left[:, 0:TT, 1], left[:, 0:TT, 0], -1.0, float(count), ALU.mult, ALU.add))
                for t in range(TT):
                    link(nc.vector.scalar_tensor_tensor(cum[:, t, n], cum[:, t, n], left[:, t, 1:2], eq[:, t, n], ALU.is_le, ALU.mult))
                link(nc.vector.tensor_tensor(out_ap, cum[:, :, n], gt[:, :, n], ALU.add))
            ones_e = te(1)
            link(nc.vector.memset(small[1], 1.0))
            dve.wait_ge(sig_exp, 1)
            dve.wait_ge(ld_bias, 16)
            sc, scb, sel = te(2), te(3), te(4)
            link(nc.vector.tensor_scalar_add(small[0], small[0], 1.0))
            link(nc.vector.reciprocal(small[2], small[0]))
            link(nc.vector.tensor_tensor(scb, sc, bias_e.unsqueeze(1).to_broadcast([P, TT, E]), ALU.add))
            quad = small[3].rearrange("p (g a b) -> p g a b", a=2, b=2)
            s2 = small[5][:, 0:32].rearrange("p (g a) -> p g a", a=2)
            m2 = small[5][:, 32:64].rearrange("p (g a) -> p g a", a=2)
            gs = small[6][:, 0:16]
            link(nc.vector.tensor_tensor(s2, quad[:, :, :, 0], quad[:, :, :, 1], ALU.add))
            link(nc.vector.tensor_tensor(m2, quad[:, :, :, 0], quad[:, :, :, 1], ALU.max))
            link(nc.vector.tensor_tensor(gs, m2[:, :, 0], m2[:, :, 1], ALU.add))
            link(nc.vector.tensor_tensor(small[6][:, 16:32], s2[:, :, 0], s2[:, :, 1], ALU.max))
            link(nc.vector.tensor_tensor(gs, gs, small[6][:, 16:32], ALU.max))
            tmp = [te(7), te(8), te(9), te(10), te(11)]
            gsel = small[6][:, 32:48]
            first(gsel.rearrange("p (t g) -> p t g", t=TT), gs.rearrange("p (t g) -> p t g", t=TT), ROUTE_GROUPS, TOP_GROUPS, tmp)
            link(nc.vector.tensor_tensor(small[12].rearrange("p (g e) -> p g e", g=TT * ROUTE_GROUPS), small[3].rearrange("p (g e) -> p g e", g=TT * ROUTE_GROUPS),
                                         gsel.unsqueeze(2).to_broadcast([P, TT * ROUTE_GROUPS, E // ROUTE_GROUPS]), ALU.mult))
            first(sel, te(12), E, TOP_EXPERTS, tmp)
            nc.vector.tensor_copy(small[13], small[4]).then_inc(sel_done, 1)
            link(nc.vector.tensor_tensor(small[5], small[2], small[4], ALU.mult))
            wsum = small[6][:, 0:2]
            link(nc.vector.reduce_sum(wsum, te(5), AX.X))
            link(nc.vector.tensor_scalar_add(wsum, wsum, 1e-20))
            link(nc.vector.reciprocal(small[6][:, 2:4], wsum))
            for t in range(TT):
                link(nc.vector.tensor_scalar(te(5)[:, t, :], te(5)[:, t, :], small[6][:, 2 + t:3 + t], ROUTE_SCALE, ALU.mult, ALU.mult))
            link(nc.vector.tensor_scalar(small[7], small[4], -1000.0, 1000.0, ALU.mult, ALU.add))
            dve.wait_ge(pos_mm, 1)
            link(nc.vector.tensor_tensor(small[7], psA[1][:, 0:TT * E], small[7], ALU.add))
            dve.wait_ge(cleared, 2)
            for t in range(TT):
                nc.vector.tensor_tensor(oh[:, t, :, 0:CAP], te(7)[:, t, :].unsqueeze(2).to_broadcast([P, E, CAP]),
                                        const[:, C_IOTA:C_IOTA + CAP].unsqueeze(1).to_broadcast([P, E, CAP]), ALU.is_equal).then_inc(oh_done, 1)
            for t in range(TT):
                dve.wait_ge(oh_done, t + 1)
                nc.vector.tensor_tensor(ow[:, t, :, 0:CAP], oh[:, t, :, 0:CAP],
                                        te(5)[:, t, :].unsqueeze(2).to_broadcast([P, E, CAP]), ALU.mult).then_inc(ow_done, 1)
            for i in range(DC):
                dve.wait_ge(sh_silu, i + 1)
                nc.vector.tensor_tensor(hs[:, i, :], psF[i % 2][:, T:2 * T], hs[:, i, :], ALU.mult).then_inc(sh_done, 1)
            for g in range(NG):
                dve.wait_ge(gu_silu, g + 1)
                nc.vector.tensor_tensor(hid[:, g % 2, :], psF[g % 2][:, FI:2 * FI], hid[:, g % 2, :], ALU.mult).then_inc(hid_done, 1)
                dve.wait_ge(y_mm, g + 1)
                wait(dve, comb_mm, g - 1)
                nc.vector.tensor_copy(y[:, g % 2, :], psA[g % 2][:, :]).then_inc(y_copied, 1)
            dve.wait_ge(comb_mm, NG)
            for st in range(TT):
                ins = nc.vector.tensor_tensor(x[:, st, :], psO[st][:, :], x[:, st, :], ALU.add)
            ins.then_inc(x3_done, 1)

        @block.tensor
        def _(pe):
            mm = nc.tensor.matmul

            def xn_transposes(n):
                for s in range(TT):
                    pe.wait_ge(ln_xn, TT * (n - 1) + s + 1)
                    for c in range(DC):
                        last = nc.tensor.transpose(psS[0][:, T * c + P * s:T * c + P * s + P], xn[:, s, P * c:P * c + P], ident)
                last.then_inc(ln_tr, 1)
            pe.wait_ge(ld_const, 16)
            xn_transposes(1)
            pe.wait_ge(ln_T, 1)
            def rope_transposes(n):
                pe.wait_ge(kr_done, n + 1)
                wait(pe, ktlo_done, n)
                for i in range(8):
                    last = nc.tensor.transpose(psS[0][:, P * i:P * i + P], kr[:, n % 2, i, :], ident)
                last.then_inc(krT_done, 1)

            def query(what, h, c=0):
                n, j = h // 2, h % 2
                w = w_pair[:, n % PAIR_BUFS, :]
                wq = w[:, 0:DC * 2 * K].rearrange("p (c k) -> p c k", c=DC)
                wk = w[:, DC * 2 * K:DC * 2 * K + 3 * 2 * K].rearrange("p (c k) -> p c k", c=3)
                wr = w[:, DC * 2 * K + 3 * 2 * K:W_PAIR].rearrange("p (c r) -> p c r", c=3)
                if what == "hk":
                    if c == 0:
                        pe.wait_ge(ld_pair[n % PAIR_BUFS], 16 * (n // PAIR_BUFS + 1))
                        wait(pe, qhk_copied, h - 1)
                    last = mm(psO[h % 2][:, 0:T], wq[:, c, K * j:K * j + K], xnT[:, c, :], start=c == 0, stop=c == DC - 1)
                    if c == DC - 1:
                        last.then_inc(qhk_mm, 1)
                elif what == "b":
                    wait(pe, qlo_done, h - 1)
                    wait(pe, qhi_done, h - 1)
                    for c in range(3):
                        last = mm(psF[h % 2][:, 0:R], wk[:, c, K * j:K * j + K], wr[:, c, R * j:R * j + R], start=c == 0, stop=c == 2)
                    last.then_inc(b_mm, 1)
                else:
                    pe.wait_ge(b_copied, h + 1)
                    pe.wait_ge(qhk_copied, h + 1)
                    mm(psF[h % 2][:, T:2 * T], b_dup[:, h % 2, :], qhk[:, h % 2, :], start=True, stop=True).then_inc(q_mm, 1)

            def aux(q, n, step):
                bank = psA[n % 2]
                wait(pe, s_free, q * AUX + n - 1)
                if step[0] == "k":
                    c = slice(512 * step[1], 512 * step[1] + 512)
                    if step[1] == 0:
                        pe.wait_ge(qmax_copied, q * 3 + 3)
                    mm(bank[:, :], wkr_now[:, 0, :], kt_hi[:, c], start=True, stop=False)
                    mm(bank[:, :], wkr_now[:, 0, :], kt_lo[:, c], start=False, stop=False)
                    mm(bank[:, :], wkr_now[:, 1, :], kt_hi[:, c], start=False, stop=True).then_inc(s_aux, 1)
                elif step[0] == "m":
                    _, c, j, st = step
                    if j == 0 and st == 0:
                        pe.wait_ge(s_khi, q * 8 + c + 1)
                    r = slice(R * j, R * j + R)
                    mm(bank[:, :], q_max[r, j, P * st:P * st + P], k_hi[r, 512 * c:512 * c + 512], start=True, stop=True).then_inc(s_aux, 1)
                else:
                    j = step[1]
                    pe.wait_ge(s_negm, q + 1)
                    for st in range(TT):
                        last = mm(bank[R:R + 1, P * st:P * st + P], negm[:, TT * j + st:TT * j + st + 1], ident_b, start=True, stop=True)
                    last.then_inc(s_aux, 1)

            def aux_part(q, s, part):
                for n, step in PLAN[s][part]:
                    aux(q, n, step)

            def scores(p, s):
                if s == SLOTS:
                    p, s = p + 1, 0
                j, g = s // HALF, s % HALF
                wait(pe, s_pf, p * SLOTS + s - 1)
                if g == 0:
                    pe.wait_ge(k_copied[j], p * 80 + 80)
                    pe.wait_ge(s_free, p * AUX + AUX - 1 + j)
                for i in range(GROUP):
                    l = slice(P * (GROUP * g + i), P * (GROUP * g + i) + P)
                    o = psS[s % 2][:, T * i:T * i + T]
                    mm(o, k1[:, j, l], q1[:, j, :], start=True, stop=False)
                    last = mm(o, k2[0:R + 1, j, l], q2[0:R + 1, j, :], start=False, stop=True)
                last.then_inc(s_scores, 1)

            def context_hi(p, s):
                g, t = s % HALF, p * SLOTS + s
                if g == 0:
                    wait(pe, s_out, p * 4 + 2 * (s // HALF))
                pe.wait_ge(s_phi, t + 1)
                for i in range(GROUP):
                    for st in range(TT):
                        mm(psO[st][:, 0:VW], p_hi[:, s % 2, T * i + P * st:T * i + P * st + P], vx[:, GROUP * g + i, :],
                           start=g == 0 and i == 0, stop=False)

            def context_lo(p, s):
                g, t = s % HALF, p * SLOTS + s
                pe.wait_ge(s_plo, t + 1)
                for i in range(GROUP):
                    for st in range(TT):
                        last = mm(psO[st][:, 0:K + 1], p_lo[:, s % 2, T * i + P * st:T * i + P * st + P], vx[:, GROUP * g + i, 0:K + 1],
                                  start=False, stop=g == HALF - 1 and i == GROUP - 1)
                last.then_inc(s_pv, 1)

            def body(p, ahead=True):
                for s in range(SLOTS):
                    if s < SLOTS - 1 or ahead:
                        scores(p, s + 1)
                    if ahead:
                        aux_part(p + 1, s, slice(0, 1))
                    context_hi(p, s)
                    if ahead:
                        aux_part(p + 1, s, slice(1, 2))
                    context_lo(p, s)
                    if ahead:
                        aux_part(p + 1, s, slice(2, None))
            for what, n, *rest in BEFORE:
                if what == "rope":
                    rope_transposes(n)
                elif what != "x":
                    query(what, n, *rest)
                else:
                    if n == 0:
                        pe.wait_ge(ktlo_done, 4)
                        pe.wait_ge(kthi_done, 4)
                        pe.wait_ge(vlo_done, 4)
                        pe.wait_ge(ident_done, 1)
                    aux(0, n, *rest)
            pe.wait_ge(qlo_done, H)
            pe.wait_ge(ones_done, 1)
            scores(0, 0)
            body(0)
            with pe.Fori(1, NPAIR - 1) as p:
                body(p)
            body(NPAIR - 1, ahead=False)
            pe.wait_ge(s_out, 2 * H)
            pe.wait_ge(ld_wkv, 16)
            pe.wait_ge(ld_wo1, 16)
            for h in range(H + 2):
                if h < H:
                    wait(pe, ct_copied, h - 1)
                    for st in range(TT):
                        last = nc.tensor.transpose(psS[0][:, 512 * (h % 2) + P * st:512 * (h % 2) + P * st + P], ctx_all[:, st, h, :], ident)
                    last.then_inc(ct_mm, 1)
                if 1 <= h <= H:
                    g = h - 1
                    pe.wait_ge(ct_copied, g + 1)
                    wait(pe, lat_copied, g - 1)
                    mm(psA[g % 2][:, 0:T], wkv[:, g, :], ctxT[:, g % 2, :], start=True, stop=True).then_inc(lat_mm, 1)
                if h >= 2:
                    g = h - 2
                    pe.wait_ge(lat_copied, g + 1)
                    for st in range(TT):
                        last = mm(psO[st][:, :], latT[:, g % 2, P * st:P * st + P], wo1[:, g, :], start=g == 0, stop=g == H - 1)
                    last.then_inc(o1_mm, 1)
            xn_transposes(2)
            pe.wait_ge(ln_T, 2)
            pe.wait_ge(ld_wa, 16)
            pe.wait_ge(lat_copied, H)
            for n, w in enumerate((w_qa, w_kva)):
                for c in range(DC):
                    last = mm(psA[n][:, 0:T], w[:, c, :], xnT[:, c, :], start=c == 0, stop=c == DC - 1)
                last.then_inc(qa_mm, 1)
            pe.wait_ge(x1_done, 1)
            for n, o in ((0, NOPE), (1, 0)):
                for c in range(DC):
                    last = mm(psO[0][0:PE2, T * n:T * n + T], w_kpe[:, c, o:o + PE2], xnT[:, c, :], start=c == 0, stop=c == DC - 1)
            last.then_inc(kpe_mm, 1)
            pe.wait_ge(qa_copied, 2)
            pe.wait_ge(ld_kvb, 16)
            for st in range(TT):
                mm(psF[st], ckv[:, P * st:P * st + P], w_vb, start=True, stop=True).then_inc(v_mm, 1)
            for n in range(NH2 // 2):
                wait(pe, kn_copied, n - 1)
                for i in range(2):
                    last = mm(psA[n % 2][PE2:QW, T * i:T * i + T], w_kb[:, 2 * n + i, :], ckv, start=True, stop=True)
                last.then_inc(kn_mm, 1)

            def queries(h):
                if h == 0:
                    pe.wait_ge(ld_qb, 16)
                wait(pe, q2_done, h - 1)
                mm(psE[h % 2][0:QW, 0:T], w_qb[:, h, NOPE:P], qa, start=True, stop=True)
                mm(psE[h % 2][0:PE2, T:2 * T], w_qb[:, h, 0:PE2], qa, start=True, stop=True).then_inc(q2_mm, 1)

            def scores2(h):
                if h == 0:
                    pe.wait_ge(v_copied, TT)
                    pe.wait_ge(kpe_spread, 1)
                    pe.wait_ge(kn_copied, NH2 // 2)
                pe.wait_ge(q2_done, h + 1)
                wait(pe, s2_max, h - 1)
                mm(psF[h % 2][:, 0:P], qf[0:QW, h, 0:P], kf[0:QW, h, 0:P], start=True, stop=True)
                mm(psF[h % 2][:, P:3 * P], qf[0:QW, h, P:T], kf[0:QW, h, :], start=True, stop=True).then_inc(s2_mm, 1)

            def transposes2(h):
                pe.wait_ge(s2_exp, 2 * h + 2)
                wait(pe, pT_copied, h - 1)
                for i in range(3):
                    last = nc.tensor.transpose(psA[h % 2][:, P * i:P * i + P], sm[:, h, P * i:P * i + P], ident)
                last.then_inc(pT_mm, 1)

            def values2(h):
                pe.wait_ge(pT_copied, h + 1)
                w = slice(V2 * h, V2 * h + V2)
                mm(psO[0][:, w], pT[:, h % 2, 0:P], v2[:, 0, w], start=True, stop=True)
                mm(psO[1][:, w], pT[:, h % 2, P:2 * P], v2[:, 0, w], start=True, stop=False)
                mm(psO[1][:, w], pT[:, h % 2, 2 * P:3 * P], v2[:, 1, w], start=False, stop=True).then_inc(o2_mm, 1)
            for h in range(NH2 + 5):
                if h < NH2:
                    queries(h)
                if 0 <= h - 1 < NH2:
                    scores2(h - 1)
                if 0 <= h - 3 < NH2:
                    transposes2(h - 3)
                if 0 <= h - 4 < NH2:
                    values2(h - 4)
            for st in range(TT):
                pe.wait_ge(o2_done, st + 1)
                for c in range(DC):
                    last = nc.tensor.transpose(psS[0][:, T * c + P * st:T * c + P * st + P], xn[:, st, P * c:P * c + P], ident)
            last.then_inc(o2T_mm, 1)
            pe.wait_ge(o2T_copied, 1)
            pe.wait_ge(ld_wo2, 16)
            for st in range(TT):
                for c in range(DC):
                    last = mm(psA[st][:, :], xnT[:, c, P * st:P * st + P], wo2[:, c, :], start=c == 0, stop=c == DC - 1)
            last.then_inc(x2_mm, 1)
            xn_transposes(3)
            pe.wait_ge(ln_T, 3)
            pe.wait_ge(ld_router, 16)
            for st in range(TT):
                for c in range(DC):
                    last = mm(psA[0][:, E * st:E * st + E], xnT[:, c, P * st:P * st + P], w_router[:, c, :], start=c == 0, stop=c == DC - 1)
            last.then_inc(logit_mm, 1)
            pe.wait_ge(ld_shared[0], 16)
            pe.wait_ge(ld_shared[1], 16)
            for i in range(DC):
                wait(pe, sh_done, i - 1)
                for n, w in enumerate((sg, su)):
                    for c in range(DC):
                        last = mm(psF[i % 2][:, T * n:T * n + T], w[:, c, P * i:P * i + P], xnT[:, c, :], start=c == 0, stop=c == DC - 1)
                last.then_inc(sh_mm, 1)
                if i == 1:
                    pe.wait_ge(sel_done, 1)
                    early, ones = const[:, C_EARLY:C_EARLY + P], const[:, C_ONES:C_ONES + P]
                    chosen = small[13].rearrange("p (t e) -> p t e", t=TT)
                    mm(psA[1][:, 0:E], early, chosen[:, 0, :], start=True, stop=True)
                    mm(psA[1][:, E:2 * E], ones, chosen[:, 0, :], start=True, stop=False)
                    mm(psA[1][:, E:2 * E], early, chosen[:, 1, :], start=False, stop=True).then_inc(pos_mm, 1)
            pe.wait_ge(ld_shared[2], 16)
            pe.wait_ge(sh_done, DC)
            for st in range(TT):
                for c in range(DC):
                    last = mm(psO[st][:, :], hs[:, c, P * st:P * st + P], sd[:, c, :], start=c == 0, stop=False)
            pe.wait_ge(oh_done, TT)
            for c in range(DC):
                wait(pe, xp_copied, c - 1)
                for st in range(TT):
                    last = mm(psE[c % 2][:, 0:E * CAP], xn[:, st, P * c:P * c + P], oh[:, st, :, 0:CAP], start=st == 0, stop=st == TT - 1)
                last.then_inc(xp_mm, 1)
            pe.wait_ge(ow_done, TT)
            for i in range(NG // 2):
                wait(pe, owT_copied, i - 1)
                for n in range(2):
                    for st in range(TT):
                        o = T * n + P * st
                        last = nc.tensor.transpose(psA[i % 2][:, o:o + P], ow[:, st, GE * (2 * i + n):GE * (2 * i + n + 1), :].rearrange("p e s -> p (e s)"), ident)
                last.then_inc(owT_mm, 1)
            pe.wait_ge(xp_copied, DC)
            pe.wait_ge(owT_copied, NG // 2)

            def gate_up(g):
                wait(pe, hid_done, g - 1)
                for j in range(GE):
                    e = GE * g + j
                    pe.wait_ge(ld_gu[e % RING], 16 * (e // RING + 1))
                for c in range(DC):
                    for j in range(GE):
                        e = GE * g + j
                        last = mm(psF[g % 2][SLOT * j:SLOT * j + SLOT, :], xpT[:, c, e, :], ring[:, e % RING, 2 * FI * c:2 * FI * (c + 1)],
                                  start=c == 0, stop=c == DC - 1)
                last.then_inc(gu_mm, 1)

            def down(g):
                pe.wait_ge(hid_done, g + 1)
                wait(pe, hT_copied, g - 1)
                for c in range(FC):
                    last = nc.tensor.transpose(psE[g % 2][:, P * c:P * c + P], hid[:, g % 2, P * c:P * c + P], ident)
                last.then_inc(hT_mm, 1)
                pe.wait_ge(hT_copied, g + 1)
                wait(pe, y_copied, g - 1)
                for j in range(GE):
                    e = GE * g + j
                    pe.wait_ge(ld_down[e % RING], 16 * (e // RING + 1))
                for c in range(FC):
                    for j in range(GE):
                        e = GE * g + j
                        o = 2 * FI * DC + D * c
                        last = mm(psA[g % 2][SLOT * j:SLOT * j + SLOT, :], hT[:, g % 2, c, SLOT * j:SLOT * j + SLOT], ring[:, e % RING, o:o + D],
                                  start=c == 0, stop=c == FC - 1)
                last.then_inc(y_mm, 1)

            def combine(g):
                pe.wait_ge(y_copied, g + 1)
                for st in range(TT):
                    last = mm(psO[st][:, :], owT[:, g, P * st:P * st + P], y[:, g % 2, :], start=False, stop=g == NG - 1)
                last.then_inc(comb_mm, 1)
            for g in range(NG):
                gate_up(g)
                down(g)
                if g:
                    combine(g - 1)
            combine(NG - 1)


def constants():
    c = np.zeros((P, C_END), np.float32)
    i = np.arange(P)
    c[:, C_ID:C_ID + P] = np.eye(P)
    causal = np.where(i[:, None] >= i[None, :], 0, NEG)
    c[:, C_MASK:C_MASK + P] = causal
    c[:, C_MASK + 2 * P:C_MASK + 3 * P] = causal
    c[:, C_EARLY:C_EARLY + P] = i[:, None] < i[None, :]
    c[:, C_ONES:C_ONES + P] = 1
    c[:, C_IOTA:C_IOTA + 16] = np.arange(16)
    inv = (np.float32(10000.0) ** (-np.arange(0, 64, 2, dtype=np.float32) / np.float32(64))).astype(np.float32)
    ang = (np.arange(T, dtype=np.float32)[:, None] * inv[None, :]).astype(np.float32)
    c[0:32, C_COS:C_COS + T] = c[32:64, C_COS:C_COS + T] = np.cos(ang).T
    c[64:96, C_COS:C_COS + T] = 1
    c[0:32, C_SIN:C_SIN + T] = -np.sin(ang).T
    c[32:64, C_SIN:C_SIN + T] = np.sin(ang).T
    inv = (np.float32(1.0) / np.float32(10000.0) ** (np.arange(0, K, 2, dtype=np.float32) / np.float32(K))).astype(np.float32)
    ang = (np.arange(L, dtype=np.float32)[:, None] * inv[None, :]).astype(np.float32)
    sin = np.sin(ang)
    sin[:, 0:32] *= -1
    rope = np.stack([np.cos(ang), sin], 1).reshape(LT, P, 2, 64).transpose(1, 0, 2, 3)
    return c, np.ascontiguousarray(rope, np.float32)


def rows(w, parts=P):
    return np.asarray(w).reshape(-1, parts, w.shape[1]).transpose(1, 0, 2)


def lay_out(i):
    g = {k: np.asarray(v) for k, v in i.items()}
    const, rope = constants()
    arrays = {"x": g["x"], "const": const, "rope": rope}
    arrays["ctx"] = g["ctx_512"].reshape(LT, P, K).transpose(1, 0, 2)
    wq = rows(g["L0_xattn_Wq"].T)
    wk = g["L0_xattn_w_kc_q"].transpose(2, 0, 1).reshape(3, P, H, K).transpose(1, 0, 2, 3)
    wr = g["L0_xattn_W_qr"].transpose(1, 0, 2).reshape(3, P, H, R).transpose(1, 0, 2, 3)
    arrays["w_pair"] = np.stack([np.concatenate([
        wq[:, :, 2 * K * n:2 * K * n + 2 * K].reshape(P, -1),
        wk[:, :, 2 * n:2 * n + 2].reshape(P, -1), wr[:, :, 2 * n:2 * n + 2].reshape(P, -1)], 1) for n in range(NPAIR)])
    arrays["w_kr"] = g["L0_xattn_W_kr"].transpose(1, 0, 2).reshape(P, H * R)
    arrays["w_kv"] = g["L0_xattn_w_kc_kv"].transpose(2, 0, 1)
    arrays["w_o1"] = rows(g["L0_xattn_Wo"].T)
    kva = g["L0_attn_Wkva"]
    kpe = kva[:, P:]
    even, odd = kpe[:, 0::2], kpe[:, 1::2]
    arrays["w_a"] = np.concatenate([rows(g["L0_attn_Wqa"]).reshape(P, -1), rows(kva[:, :P]).reshape(P, -1),
                                    rows(np.concatenate([odd, even, odd], 1)).reshape(P, -1)], 1)
    qb = g["L0_attn_Wqb"].reshape(P, NH2, QW)
    pe = qb[:, :, NOPE:]
    arrays["w_qb"] = np.concatenate([pe[:, :, 1::2], pe[:, :, 0::2], pe[:, :, 1::2], qb[:, :, :NOPE]], 2)
    kvb = g["L0_attn_Wkvb"].reshape(P, NH2, NOPE + V2)
    arrays["w_kvb"] = np.concatenate([kvb[:, :, :NOPE].reshape(P, -1), kvb[:, :, NOPE:].reshape(P, -1)], 1)
    arrays["w_o2"] = rows(g["L0_attn_Wo"])
    arrays["w_router"] = rows(g["L0_ffn_router_w"].T)
    arrays["e_bias"] = g["L0_ffn_e_bias"]
    arrays["w_shared"] = np.stack([rows(g[f"L0_ffn_shared_{n}"].T) for n in ("gate", "up", "down")])
    up = [g[f"L0_ffn_W_{n}"].reshape(E, DC, P, FI) for n in ("gate", "up")]
    down = g["L0_ffn_W_down"].reshape(E, FC, P, D).transpose(0, 2, 1, 3).reshape(E, P, -1)
    arrays["w_exp"] = np.concatenate([np.concatenate(up, 3).transpose(0, 2, 1, 3).reshape(E, P, -1), down], 2)
    return {k: np.ascontiguousarray(v) for k, v in arrays.items()}


def kernel(**inputs):
    import concourse.bacc as bacc
    from concourse.bass_utils import run_bass_kernel_spmd

    nc = bacc.Bacc("TRN2", target_bir_lowering=False, num_devices=1)
    arrays = lay_out(inputs)
    aps = {n: nc.dram_tensor(n, v.shape, F32, kind="ExternalInput").ap() for n, v in arrays.items()}
    out = nc.dram_tensor("out", (1, T, D), F32, kind="ExternalOutput").ap()
    layer(nc, aps, out)
    r = run_bass_kernel_spmd(nc, [arrays], core_ids=[0])
    return r.results[0]["out"]
```

```python
from contextlib import ExitStack

import numpy as np

import concourse.bass as bass
from concourse import mybir

F32 = mybir.dt.float32
BF16 = mybir.dt.bfloat16
ACT = mybir.ActivationFunctionType
ALU = mybir.AluOpType
AX = mybir.AxisListType

P = 128
T = 256
TT = T // P
D = 512
DC = D // P
L = 4096
LT = L // P
H = 16
NPAIR = H // 2
K = 128
CQ = 384
R = 64
GROUP = 4
SLOTS = 2 * LT // GROUP
HALF = SLOTS // 2
VW = 2 * K + 1
NH2 = 16
PE2, NOPE = 64, 32
QW = PE2 + NOPE
V2 = 32
E = 32
FI = 256
FC = FI // P
CAP = 10
SLOT = 32
GE = P // SLOT
NG = E // GE
W_GU = DC * 2 * FI
W_EXP = W_GU + FC * D
RING = 11
RING_LOW = 8
QK_BUFS, SM_BUFS = 4, 5
SH_EARLY = 2
XPW = E * CAP + SLOT - CAP
ROUTE_GROUPS, TOP_GROUPS, TOP_EXPERTS, ROUTE_SCALE = 8, 3, 4, 2.5
NEG = -3.0e38
EPS = 1e-5

C_ID, C_MASK, C_EARLY, C_ONES, C_IOTA, C_COS, C_SIN = 0, 128, 512, 640, 768, 784, 1040
C_END = 1296
W_PAIR = DC * 2 * K + (CQ // P) * 2 * K + (CQ // P) * 2 * R


def aux_plan():
    keys = [("k", c) for c in range(8)]
    maxima = [("m", c, j, st) for c in range(8) for j in range(2) for st in range(TT)]
    plan = [[] for _ in range(SLOTS)]
    for s in range(8):
        plan[s] = [keys.pop(0)] + [maxima.pop(0) for _ in range(2 if s else 0)]
    for s in range(8, 14):
        plan[s] = [maxima.pop(0) for _ in range(3)]
    plan[14] = [("t", 0), ("t", 1)]
    n = 0
    for s in range(SLOTS):
        for i, step in enumerate(plan[s]):
            plan[s][i] = (n, step)
            n += 1
    return plan, n


PLAN, AUX = aux_plan()
LAST_KEY = max(n for s in PLAN for n, step in s if step[0] == "k")
LAST_MAX = max(n for s in PLAN for n, step in s if step[0] == "m")


def before_loop():
    pieces = []
    for h in range(H + 1):
        if h < H:
            pieces += [("hk", h, c) for c in range(DC)] + [("b", h)]
        if h:
            pieces.append(("e", h - 1))
    steps = [("x", n, step) for slot in PLAN for n, step in slot]
    order, pieces = pieces[:ROPE_AFTER], pieces[ROPE_AFTER:]
    for n in range(4):
        order += [("rope", n)] + pieces[:PER_ROPE]
        pieces = pieces[PER_ROPE:]
    while pieces:
        order.append(pieces.pop(0))
        if len(steps) > 2:
            order.append(steps.pop(0))
    return order + steps


ROPE_AFTER, PER_ROPE = 18, 8
BEFORE = before_loop()
PAIR_BUFS = 6


def wait(eng, sem, value):
    if isinstance(value, int) and value <= 0:
        return
    eng.wait_ge(sem, value)


def wait_apart(eng, sem, value, passed):
    if not isinstance(value, int):
        eng.wait_ge(sem, value)
        eng.sem_inc(passed, 1)
    else:
        wait(eng, sem, value)


def layer(nc, a, out, stage=3):
    with ExitStack() as ctx:
        def sb(name, shape, dt=F32):
            return ctx.enter_context(nc.sbuf_tensor(name, shape, dt))

        def ps(name, cols):
            return ctx.enter_context(nc.psum_tensor(name, [P, cols], F32))

        def sem(name):
            return ctx.enter_context(nc.semaphore(name))

        top = [0]
        arena = sb("arena", [P, 53100])

        def cut(cols, at=None):
            o = top[0] if at is None else at
            if at is None:
                top[0] += cols
            return arena[:, o:o + cols]

        vx = cut(LT * VW // 2).bitcast(BF16).rearrange("p (t w) -> p t w", w=VW)
        kt_hi = cut(L // 2).bitcast(BF16)
        kt_lo = cut(L // 2).bitcast(BF16)
        stage_at = top[0]
        k_hi = cut(L // 2).bitcast(BF16)
        k_lo = cut(L // 2).bitcast(BF16)
        k1_at = top[0]
        k1 = cut(L).bitcast(BF16).rearrange("p (j l) -> p j l", j=2)
        k2_at = top[0]
        k2 = cut(L).bitcast(BF16).rearrange("p (j l) -> p j l", j=2)
        p_f = cut(2048).rearrange("p (b n) -> p b n", b=2)
        p_hi = cut(1024).bitcast(BF16).rearrange("p (b n) -> p b n", b=2)
        p_lo = cut(1024).bitcast(BF16).rearrange("p (b n) -> p b n", b=2)
        q_at = top[0]
        q1_all = cut(H * T // 2).bitcast(BF16).rearrange("p (h s) -> p h s", h=H)
        q2_all = cut(H * T // 2).bitcast(BF16).rearrange("p (h s) -> p h s", h=H)
        r_at = top[0]
        wkv = cut(H * K).rearrange("p (h k) -> p h k", h=H)
        wo1 = cut(H * D).rearrange("p (h n) -> p h n", h=H)
        ctx_all = cut(TT * H * K).rearrange("p (s h d) -> p s h d", s=TT, h=H)
        x = cut(TT * D).rearrange("p (s d) -> p s d", s=TT)
        xn = cut(TT * D).rearrange("p (s d) -> p s d", s=TT)
        xnT = cut(DC * T).rearrange("p (c s) -> p c s", c=DC)
        const = cut(C_END)
        w_at = top[0]
        wkr_hi = cut(512).bitcast(BF16)
        wkr_lo = cut(512).bitcast(BF16)
        wkr_now = cut(128).bitcast(BF16).rearrange("p (b n) -> p b n", b=2)
        q_max = cut(256).bitcast(BF16).rearrange("p (j s) -> p j s", j=2)
        q1 = cut(256).bitcast(BF16).rearrange("p (j s) -> p j s", j=2)
        q2 = cut(256).bitcast(BF16).rearrange("p (j s) -> p j s", j=2)
        ident_b = cut(64).bitcast(BF16)
        bn = cut(16)
        mv = cut(8)
        maxes = cut(32).rearrange("p (j s c) -> p (j s) c", j=2, s=TT)
        mx4 = cut(4)
        negm = cut(2).bitcast(BF16)
        rsum = cut(2)
        ctx_in = arena[:, k1_at:k1_at + L].rearrange("p (t d) -> p t d", t=LT)
        rope = arena[:, k2_at:k2_at + L].rearrange("p (t c i) -> p t c i", t=LT, c=2)
        kr = arena[:, stage_at:stage_at + 2048].rearrange("p (b t d) -> p b t d", b=2, t=8)
        kr2 = arena[:, stage_at + 2048:stage_at + 4096].rearrange("p (b t d) -> p b t d", b=2, t=8)
        w_pair = arena[:, r_at:r_at + PAIR_BUFS * W_PAIR].rearrange("p (b n) -> p b n", b=PAIR_BUFS)
        wkr_in = arena[:, r_at + PAIR_BUFS * W_PAIR:r_at + PAIR_BUFS * W_PAIR + H * R]
        b_dup = arena[:, r_at + 14080:r_at + 14336].rearrange("p (b n) -> p b n", b=2)
        ctxT = arena[:, q_at + 3072:q_at + 3584].rearrange("p (b n) -> p b n", b=2)
        latT = arena[:, q_at + 3584:q_at + 4096].rearrange("p (b n) -> p b n", b=2)

        w_qb = arena[:, q_at:q_at + 2048].rearrange("p (h w) -> p h w", h=NH2)
        w_kvb = arena[:, q_at + 2048:q_at + 3072]
        w_kb = w_kvb[:, 0:512].rearrange("p (h w) -> p h w", h=NH2)
        w_vb = w_kvb[:, 512:1024]
        qa = arena[:, q_at + 3072:q_at + 3328]
        ckv = arena[:, q_at + 3328:q_at + 3584]
        rope_b = arena[:, q_at + 3584:q_at + 4096].rearrange("p (b n) -> p b n", b=2)
        wa_at = top[0]
        w_a = cut(DC * (P + P + 3 * V2))
        w_qa = w_a[:, 0:512].rearrange("p (c n) -> p c n", c=DC)
        w_kva = w_a[:, 512:1024].rearrange("p (c n) -> p c n", c=DC)
        w_kpe = w_a[:, 1024:1408].rearrange("p (c n) -> p c n", c=DC)
        qhk = arena[:, top[0]:top[0] + 2 * T].rearrange("p (b n) -> p b n", b=2)
        raw = arena[:, top[0]:top[0] + TT * VW].rearrange("p (s w) -> p s w", s=TT)
        wo2 = cut(DC * D).rearrange("p (c n) -> p c n", c=DC)
        high_at = r_at + (RING - RING_LOW) * W_EXP
        qk = arena[:, high_at:high_at + QK_BUFS * 2 * T].rearrange("p (h n) -> p h n", h=QK_BUFS)
        sm = arena[:, high_at + QK_BUFS * 2 * T:high_at + QK_BUFS * 2 * T + SM_BUFS * 3 * P].rearrange("p (h n) -> p h n", h=SM_BUFS)
        pT = arena[:, w_at:w_at + 768].rearrange("p (b n) -> p b n", b=2)
        v2 = arena[:, w_at + 768:w_at + 1792].rearrange("p (s n) -> p s n", s=TT)
        negm2 = arena[:, w_at + 1792:w_at + 1824].rearrange("p (h s) -> p h s", h=NH2)
        sums2 = arena[:, w_at + 1824:w_at + 1856].rearrange("p (s h) -> p s h", h=NH2)
        rsum2 = arena[:, w_at + 1856:w_at + 1888].rearrange("p (s h) -> p s h", h=NH2)

        ring = [arena[:, o:o + W_EXP] for o in [W_EXP * e for e in range(RING_LOW)]
                + [r_at + W_EXP * e for e in range(RING - RING_LOW)]]
        w_router = cut(DC * E).rearrange("p (c e) -> p c e", c=DC)
        bias_e = cut(E)
        sg = arena[:, high_at:high_at + 2048].rearrange("p (c n) -> p c n", c=DC)
        su = arena[:, high_at + 2048:high_at + 4096].rearrange("p (c n) -> p c n", c=DC)
        hs = arena[:, high_at + 4096:high_at + 5120].rearrange("p (c t) -> p c t", c=DC)
        sd = arena[:, wa_at:wa_at + 2048].rearrange("p (c n) -> p c n", c=DC)
        xpT = arena[:, wa_at + 2048:wa_at + 2048 + DC * XPW].rearrange("p (c n) -> p c n", c=DC)
        ow = arena[:, q_at:q_at + 2048].rearrange("p (t e s) -> p t e s", t=TT, e=E)
        owT = arena[:, q_at + 2048:q_at + 4096].rearrange("p (g t) -> p g t", g=NG)
        y = xn
        oh = arena[:, w_at:w_at + TT * E * CAP].rearrange("p (t n) -> p t n", t=TT)
        hid = arena[:, w_at:w_at + 512].rearrange("p (b n) -> p b n", b=2)
        hT = arena[:, w_at + 512:w_at + 1024].rearrange("p (b c n) -> p b c n", b=2, c=FC)
        small = [arena[:, w_at + 1024 + 64 * i:w_at + 1088 + 64 * i] for i in range(14)]

        ident = const[:, C_ID:C_ID + P]

        psS = [ps(f"psS{i}", 1024) for i in range(2)]
        psO = [ps(f"psO{i}", 512) for i in range(2)]
        psA = [ps(f"psA{i}", 512) for i in range(2)]
        psE = [psS[0][:, 0:512], psS[0][:, 512:1024]]
        psF = [psS[1][:, 0:512], psS[1][:, 512:1024]]
        sh_bank = [psF[0], psF[1], psO[0], psO[1]]

        ld_x, ld_const, ld_ctx, ld_rope, ld_wkr = (sem(n) for n in ("ld_x", "ld_const", "ld_ctx", "ld_rope", "ld_wkr"))
        ld_pair = [sem(f"ld_pair{i}") for i in range(PAIR_BUFS)]
        ld_wkv, ld_wo1 = sem("ld_wkv"), sem("ld_wo1")
        dve_step, act_step = sem("dve_step"), sem("act_step")
        ident_done = sem("ident_done")
        ln_var, ln_std, ln_xn, ln_tr, ln_T = (sem(n) for n in ("ln_var", "ln_std", "ln_xn", "ln_tr", "ln_T"))
        rot_done, kr_done, vhi_done, vlo_done, krT_done, kthi_done, ktlo_done = (
            sem(n) for n in ("rot_done", "kr_done", "vhi_done", "vlo_done", "krT_done", "kthi_done", "ktlo_done"))
        ones_done, wkr_split = sem("ones_done"), sem("wkr_split")
        b_mm, b_copied, qhk_mm, qhk_copied, q_mm, qhi_done, qlo_done = (
            sem(n) for n in ("b_mm", "b_copied", "qhk_mm", "qhk_copied", "q_mm", "qhi_done", "qlo_done"))
        s_scores, s_phi, s_pf, s_plo, s_pv, s_out = (
            sem(n) for n in ("s_scores", "s_phi", "s_pf", "s_plo", "s_pv", "s_out"))
        s_aux, s_khi, s_free, s_negm, s_mx, s_rsum = (sem(n) for n in ("s_aux", "s_khi", "s_free", "s_negm", "s_mx", "s_rsum"))
        k_copied = [sem(f"k_copied{j}") for j in range(2)]
        qmax_copied = sem("qmax_copied")
        ctx_sum, ctx_done = sem("ctx_sum"), sem("ctx_done")
        ct_mm, ct_copied, lat_mm, lat_copied, o1_mm, x1_done = (
            sem(n) for n in ("ct_mm", "ct_copied", "lat_mm", "lat_copied", "o1_mm", "x1_done"))
        stored = sem("stored")
        ld_wa, ld_wo2, ld_qb, ld_kvb, ld_router, ld_bias = (
            sem(n) for n in ("ld_wa", "ld_wo2", "ld_qb", "ld_kvb", "ld_router", "ld_bias"))
        qa_mm, qa_copied, kpe_mm, kpe_done, kpe_spread, qk_copied, v_mm, v_copied = (
            sem(n) for n in ("qa_mm", "qa_copied", "kpe_mm", "kpe_done", "kpe_spread", "qk_copied", "v_mm", "v_copied"))
        q2_mm, q2_done, s2_mm, s2_max, s2_exp, pT_mm, pT_copied, o2_mm, o2_done, o2T_mm, o2T_copied, x2_mm, x2_done = (
            sem(n) for n in ("q2_mm", "q2_done", "s2_mm", "s2_max", "s2_exp", "pT_mm", "pT_copied", "o2_mm", "o2_done",
                             "o2T_mm", "o2T_copied", "x2_mm", "x2_done"))
        ld_shared = [sem(f"ld_shared{i}") for i in range(3)]
        ld_gu = [sem(f"ld_gu{i}") for i in range(RING)]
        ld_down = [sem(f"ld_down{i}") for i in range(RING)]
        cleared, logit_mm, sig_exp, sel_done, pos_mm, oh_done, ow_done, xp_mm, xp_copied, owT_mm, owT_copied = (
            sem(n) for n in ("cleared", "logit_mm", "sig_exp", "sel_done", "pos_mm", "oh_done", "ow_done", "xp_mm",
                             "xp_copied", "owT_mm", "owT_copied"))
        sh_mm, sh_silu, sh_done, gu_mm, gu_silu, hid_done, hT_mm, hT_copied, y_mm, y_copied, comb_mm, x3_done = (
            sem(n) for n in ("sh_mm", "sh_silu", "sh_done", "gu_mm", "gu_silu", "hid_done", "hT_mm", "hT_copied",
                             "y_mm", "y_copied", "comb_mm", "x3_done"))
        sp_passed, pool_passed = sem("sp_passed"), sem("pool_passed")

        block = ctx.enter_context(nc.Block())

        @block.sync
        def _(sp):
            sp.dma_start(x, a["x"].rearrange("a (s p) d -> p (a s) d", p=P)).then_inc(ld_x, 16)
            sp.dma_start(const, a["const"]).then_inc(ld_const, 16)
            for n in range(2):
                sp.dma_start(w_pair[:, n, :], a["w_pair"][n]).then_inc(ld_pair[n], 16)
            sp.dma_start(ctx_in, a["ctx"]).then_inc(ld_ctx, 16)
            sp.dma_start(rope, a["rope"]).then_inc(ld_rope, 16)
            for n in range(2, NPAIR):
                if n >= PAIR_BUFS:
                    sp.wait_ge(b_mm, 2 * (n - PAIR_BUFS + 1))
                sp.dma_start(w_pair[:, n % PAIR_BUFS, :], a["w_pair"][n]).then_inc(ld_pair[n % PAIR_BUFS], 16)
                if n == 2:
                    sp.dma_start(wkr_in, a["w_kr"]).then_inc(ld_wkr, 16)

            def copy_keys(q):
                for j in range(2):
                    src = slice(R * j, R * j + R)
                    wait_apart(sp, s_free, q * AUX + LAST_KEY + 1, sp_passed)
                    wait_apart(sp, s_scores, (q - 1) * SLOTS + HALF * (j + 1), sp_passed)
                    sp.dma_start(k1[0:R, j, :], k_hi[src, :]).then_inc(k_copied[j], 16)
                    sp.dma_start(k1[R:2 * R, j, :], k_lo[src, :]).then_inc(k_copied[j], 16)
                    sp.dma_start(k2[0:R, j, :], k_hi[src, :]).then_inc(k_copied[j], 16)
                    sp.dma_start(q1[:, j, :], q1_all[:, bass.ds(q * 2 + j, 1), :].rearrange("p a s -> p (a s)")).then_inc(k_copied[j], 16)
                    sp.dma_start(q2[0:R, j, :], q2_all[0:R, bass.ds(q * 2 + j, 1), :].rearrange("p a s -> p (a s)")).then_inc(k_copied[j], 16)
            sp.wait_ge(qhi_done, 2)
            sp.wait_ge(qlo_done, 2)
            copy_keys(0)
            sp.wait_ge(qhi_done, H)
            sp.wait_ge(qlo_done, H)
            sp.dma_start(w_a, a["w_a"]).then_inc(ld_wa, 16)
            sp.dma_start(w_router, a["w_router"]).then_inc(ld_router, 16)
            sp.dma_start(bias_e, a["e_bias"].partition_broadcast(P)).then_inc(ld_bias, 16)
            sp.dma_start(wkv, a["w_kv"]).then_inc(ld_wkv, 16)
            sp.dma_start(wo1, a["w_o1"]).then_inc(ld_wo1, 16)
            with sp.Fori(1, NPAIR) as q:
                copy_keys(q)
            sp.wait_ge(s_pv, NPAIR * SLOTS)
            sp.dma_start(w_qb, a["w_qb"]).then_inc(ld_qb, 16)
            sp.dma_start(w_kvb, a["w_kvb"]).then_inc(ld_kvb, 16)
            sp.wait_ge(ctx_done, H)
            sp.dma_start(wo2, a["w_o2"]).then_inc(ld_wo2, 16)

            def load_expert(e, part, done):
                sp.dma_start(ring[e % RING][:, part], a["w_exp"][e][:, part]).then_inc(done[e % RING], 16)
            gate_up, down = slice(0, W_GU), slice(W_GU, W_EXP)
            for e in range(RING):
                if e == RING_LOW:
                    sp.wait_ge(o1_mm, H)
                load_expert(e, gate_up, ld_gu)
                load_expert(e, down, ld_down)
            sp.wait_ge(pT_mm, NH2)
            for i, w in enumerate((sg, su)):
                sp.dma_start(w, a["w_shared"][i]).then_inc(ld_shared[i], 16)
            sp.wait_ge(x2_mm, 1)
            sp.dma_start(sd, a["w_shared"][2]).then_inc(ld_shared[2], 16)
            for g in range((E - RING + GE - 1) // GE):
                block_e = range(RING + GE * g, min(RING + GE * (g + 1), E))
                sp.wait_ge(gu_mm, g + 1)
                for e in block_e:
                    load_expert(e, gate_up, ld_gu)
                sp.wait_ge(y_mm, g + 1)
                for e in block_e:
                    load_expert(e, down, ld_down)
            sp.wait_ge(x3_done, 1)
            sp.dma_start(out.rearrange("a (s p) d -> p (a s) d", p=P), x).then_inc(stored, 16)
            sp.wait_ge(stored, 16)

        @block.gpsimd
        def _(pool):
            for n in range(4):
                if n == 0:
                    pool.wait_ge(ld_ctx, 16)
                    pool.wait_ge(ld_rope, 16)
                wait(pool, kr_done, n - 1)
                t = slice(8 * n, 8 * n + 8)
                for half in range(2):
                    sin = rope[:, t, 1, 32 * half:32 * half + 32].unsqueeze(3).to_broadcast([P, 8, 32, 2])
                    o = slice(64 * half, 64 * half + 64)
                    i = slice(64 - 64 * half, 128 - 64 * half)
                    nc.gpsimd.tensor_tensor(kr2[:, n % 2, :, o].rearrange("p t (i e) -> p t i e", e=2),
                                            ctx_in[:, t, i].rearrange("p t (i e) -> p t i e", e=2),
                                            sin, ALU.mult).then_inc(rot_done, 1)

            def bring(q):
                wait_apart(pool, s_aux, (q - 1) * AUX + LAST_MAX + 1, pool_passed)
                h = q * 2
                nc.gpsimd.tensor_copy(q_max, q1_all[:, bass.ds(h, 2), :]).then_inc(qmax_copied, 1)
                nc.gpsimd.tensor_copy(wkr_now[:, 0, :], wkr_hi[:, bass.ds(q * P, P)]).then_inc(qmax_copied, 1)
                nc.gpsimd.tensor_copy(wkr_now[:, 1, :], wkr_lo[:, bass.ds(q * P, P)]).then_inc(qmax_copied, 1)
            pool.wait_ge(qhi_done, 2)
            pool.wait_ge(wkr_split, 2)
            bring(0)
            pool.wait_ge(kr_done, 4)
            pool.wait_ge(qmax_copied, 3)
            one2 = float(np.array([0x3F803F80], np.uint32).view(np.float32)[0])
            nc.gpsimd.memset(arena[R:R + 1, k2_at:k2_at + L], one2).then_inc(ones_done, 1)
            pool.wait_ge(ones_done, 1)

            def normalise(h):
                o = ctx_all[:, :, bass.ds(h, 1), :].rearrange("p s a d -> p (s a) d")
                wait_apart(pool, s_rsum, h + 1, pool_passed)
                nc.gpsimd.tensor_tensor(o, raw[:, :, 0:K], raw[:, :, K + 1:VW], ALU.add).then_inc(ctx_sum, 1)
                wait_apart(pool, ctx_sum, h + 1, pool_passed)
                nc.gpsimd.tensor_tensor(o, o, rsum.unsqueeze(2).to_broadcast([P, TT, K]), ALU.mult).then_inc(ctx_done, 1)
            pool.wait_ge(qhi_done, H)
            bring(1)
            normalise(0)
            with pool.Fori(2, NPAIR) as q:
                bring(q)
                normalise(q * 2 - 3)
                normalise(q * 2 - 2)
            for h in range(H - 3, H):
                normalise(h)
            pool.wait_ge(q2_mm, NH2)
            nc.gpsimd.memset(arena[:, q_at:q_at + 2048], 0.0).then_inc(cleared, 1)
            pool.wait_ge(x2_mm, 1)
            nc.gpsimd.memset(xpT[:, :, E * CAP:XPW], 0.0).then_inc(cleared, 1)

        @block.scalar
        def _(act):
            def std(n):
                act.wait_ge(ln_var, n)
                nc.scalar.activation(mv.rearrange("p (s c) -> p s c", c=4)[:, 0:TT, 2], mv.rearrange("p (s c) -> p s c", c=4)[:, 0:TT, 1], ACT.Sqrt).then_inc(ln_std, 1)
                for s in range(TT):
                    act.wait_ge(ln_tr, TT * (n - 1) + s + 1)
                    nc.scalar.copy(xnT[:, :, P * s:P * s + P], psE[s].rearrange("p (c s) -> p c s", c=DC)).then_inc(ln_T, 1)
            std(1)
            def rope_high(n):
                act.wait_ge(kr_done, n + 1)
                nc.scalar.copy(vx[:, 8 * n:8 * n + 8, 0:K], kr[:, n % 2]).then_inc(vhi_done, 1)
                act.wait_ge(krT_done, n + 1)
                nc.scalar.copy(kt_hi[:, 1024 * n:1024 * n + 1024], psS[0][:, :]).then_inc(kthi_done, 1)
                if n == 0:
                    act.wait_ge(ld_wkr, 16)
                    nc.scalar.copy(wkr_hi, wkr_in).then_inc(wkr_split, 1)

            def query(what, h):
                if what == "hk":
                    act.wait_ge(qhk_mm, h + 1)
                    wait(act, q_mm, h - 1)
                    nc.scalar.copy(qhk[:, h % 2, :], psO[h % 2][:, 0:T]).then_inc(qhk_copied, 1)
                elif what == "b":
                    act.wait_ge(b_mm, h + 1)
                    nc.scalar.copy(b_dup[:, h % 2, :].rearrange("p (a r) -> p a r", a=2),
                                   psF[h % 2][:, 0:R].unsqueeze(1).to_broadcast([P, 2, R])).then_inc(b_copied, 1)
                else:
                    act.wait_ge(q_mm, h + 1)
                    nc.scalar.copy(q1_all[:, h, :], psF[h % 2][:, T:2 * T]).then_inc(qhi_done, 1)

            def aux(q, n, step):
                if step[0] == "k":
                    act.wait_ge(s_aux, q * AUX + n + 1)
                    wait(act, k_copied[0], q * 80)
                    wait(act, k_copied[1], q * 80)
                    nc.scalar.copy(k_hi[:, 512 * step[1]:512 * step[1] + 512], psA[n % 2][:, :]).then_inc(s_khi, 1)
                elif step[0] == "t":
                    act.wait_ge(s_aux, q * AUX + n + 1)
                    nc.scalar.copy(q2[R:R + 1, step[1], :], psA[n % 2][R:R + 1, 0:T]).then_inc(s_free, 1)

            def head_out(p, j):
                hd = p * 2 + j
                act.wait_ge(s_pv, hd * HALF + HALF)
                wait(act, ctx_done, hd)
                for st in range(TT):
                    nc.scalar.copy(raw[:, st, :], psO[st][:, 0:VW]).then_inc(s_out, 1)

            def body(p, ahead=True):
                for s in range(SLOTS):
                    t = p * SLOTS + s
                    act.wait_ge(s_scores, t + 1)
                    wait(act, s_pv, t - 1)
                    nc.scalar.activation(p_hi[:, s % 2, :], psS[s % 2][:, :], ACT.Exp).then_inc(s_phi, 1)
                    wait(act, s_plo, t - 1)
                    nc.scalar.activation(p_f[:, s % 2, :], psS[s % 2][:, :], ACT.Exp).then_inc(s_pf, 1)
                    if s == HALF:
                        head_out(p, 0)
                    if s == 0 and not (isinstance(p, int) and p == 0):
                        head_out(p - 1, 1)
                    if ahead:
                        for n, step in PLAN[s]:
                            aux(p + 1, n, step)
            for what, n, *rest in BEFORE:
                if what == "rope":
                    rope_high(n)
                elif what == "x":
                    aux(0, n, *rest)
                elif what != "hk" or rest[0] == DC - 1:
                    query(what, n)
            body(0)
            with act.Fori(1, NPAIR - 1) as p:
                body(p)
            body(NPAIR - 1, ahead=False)
            head_out(NPAIR - 1, 1)
            for h in range(H):
                act.wait_ge(ct_mm, h + 1)
                wait(act, lat_mm, h - 1)
                nc.scalar.copy(ctxT[:, h % 2, :], psS[0][:, 512 * (h % 2):512 * (h % 2) + T]).then_inc(ct_copied, 1)
            std(2)
            act.wait_ge(qa_mm, 1)
            nc.scalar.copy(qa, psA[0][:, 0:T]).then_inc(qa_copied, 1)
            act.wait_ge(qa_mm, 2)
            nc.scalar.copy(ckv, psA[1][:, 0:T]).then_inc(qa_copied, 1)

            def nope_part(h):
                act.wait_ge(q2_mm, h + 1)
                wait(act, s2_mm, h - QK_BUFS + 1)
                nc.scalar.copy(qk[PE2:QW, h % QK_BUFS, :], psE[h % 2][PE2:QW, :]).then_inc(qk_copied, 1)
                if h == 0:
                    for st in range(TT):
                        act.wait_ge(v_mm, st + 1)
                        nc.scalar.copy(v2[:, st, :], psA[st][:, :]).then_inc(v_copied, 1)

            def exps(h):
                m = sm[:, h % SM_BUFS, :]
                act.wait_ge(s2_max, h + 1)
                nc.scalar.activation(m[:, 0:P], m[:, 0:P], ACT.Exp, bias=negm2[:, h, 0:1],
                                     accum_out=sums2[:, 0, h:h + 1]).then_inc(s2_exp, 1)
                nc.scalar.activation(m[:, P:3 * P], m[:, P:3 * P], ACT.Exp, bias=negm2[:, h, 1:2],
                                     accum_out=sums2[:, 1, h:h + 1]).then_inc(s2_exp, 1)

            def weights_back(h):
                act.wait_ge(pT_mm, h + 1)
                wait(act, o2_mm, h - 1)
                nc.scalar.copy(pT[:, h % 2, :], psA[h % 2][:, 0:3 * P]).then_inc(pT_copied, 1)
            act.wait_ge(kpe_done, 1)
            nc.scalar.copy(qk[0:PE2, 1:QK_BUFS, T:2 * T], qk[0:PE2, 0:1, T:2 * T].to_broadcast([PE2, QK_BUFS - 1, T])).then_inc(kpe_spread, 1)
            for i in range(NH2 + 3):
                if i < NH2:
                    nope_part(i)
                if i >= 3:
                    weights_back(i - 3)
                if 0 <= i - 1 < NH2:
                    exps(i - 1)
            act.wait_ge(o2T_mm, 1)
            nc.scalar.copy(xnT.rearrange("p c s -> p (c s)"), psS[0][:, :]).then_inc(o2T_copied, 1)
            std(3)

            def group_silu(g):
                act.wait_ge(gu_mm, g + 1)
                wait(act, hT_mm, g - 1)
                nc.scalar.activation(hid[:, g % 2, :], psF[g % 2][:, 0:FI], ACT.Silu).then_inc(gu_silu, 1)

            def group_back(g):
                act.wait_ge(hT_mm, g + 1)
                wait(act, y_mm, g - 1)
                nc.scalar.copy(hT[:, g % 2].rearrange("p c n -> p (c n)"), psE[g % 2][:, 0:FI]).then_inc(hT_copied, 1)

            def weights_by_slot():
                for i in range(NG // 2):
                    act.wait_ge(owT_mm, i + 1)
                    nc.scalar.copy(owT[:, 2 * i:2 * i + 2, :].rearrange("p g t -> p (g t)"), psA[i % 2][:, :]).then_inc(owT_copied, 1)
            act.wait_ge(logit_mm, 1)
            nc.scalar.activation(small[0], psA[0][:, 0:TT * E], ACT.Exp, scale=-1.0).then_inc(sig_exp, 1)
            for i in range(DC):
                if i == SH_EARLY:
                    for c in range(DC):
                        act.wait_ge(xp_mm, c + 1)
                        nc.scalar.copy(xpT[:, c, 0:E * CAP], psE[c % 2][:, 0:E * CAP]).then_inc(xp_copied, 1)
                    group_silu(0)
                    weights_by_slot()
                    group_back(0)
                act.wait_ge(sh_mm, i + 1)
                nc.scalar.activation(hs[:, i, :], sh_bank[i][:, 0:T], ACT.Silu).then_inc(sh_silu, 1)
            for g in range(1, NG):
                group_silu(g)
                group_back(g)
        @block.vector
        def _(dve):
            def low_query(h):
                dve.wait_ge(qhi_done, h + 1)
                nc.vector.tensor_tensor(q2_all[0:R, h, :], psF[h % 2][0:R, T:2 * T], q1_all[0:R, h, :], ALU.subtract).then_inc(qlo_done, 1)

            steps = [0]

            def link(ins):
                steps[0] += 1
                ins.then_inc(dve_step, 1)
                dve.wait_ge(dve_step, steps[0])

            def layernorm(n):
                st = bn[:, 0:12].rearrange("p (s c) -> p s c", c=6)
                m = mv.rearrange("p (s c) -> p s c", c=4)
                for s in range(TT):
                    link(nc.vector.bn_stats(st[:, s, :], x[:, s, :]))
                for s in range(TT):
                    link(nc.vector.bn_aggr(m[:, s, 0:2], st[:, s, :]))
                nc.vector.tensor_scalar_add(m[:, 0:TT, 1], m[:, 0:TT, 1], EPS).then_inc(ln_var, 1)
                dve.wait_ge(ln_std, n)
                link(nc.vector.reciprocal(m[:, 0:TT, 3], m[:, 0:TT, 2]))
                for s in range(TT):
                    nc.vector.tensor_scalar(xn[:, s, :], x[:, s, :], m[:, s, 0:1], m[:, s, 3:4],
                                            ALU.subtract, ALU.mult).then_inc(ln_xn, 1)
            dve.wait_ge(ld_const, 16)
            nc.vector.tensor_copy(ident_b, ident).then_inc(ident_done, 1)
            link(nc.vector.memset(vx[:, :, K:K + 1], 1.0))
            dve.wait_ge(ld_x, 16)
            layernorm(1)
            def rope_rows(n):
                t = slice(8 * n, 8 * n + 8)
                if n == 0:
                    dve.wait_ge(ld_ctx, 16)
                    dve.wait_ge(ld_rope, 16)
                wait(dve, vhi_done, n - 1)
                wait(dve, krT_done, n - 1)
                link(nc.vector.tensor_tensor(kr[:, n % 2].rearrange("p t (i e) -> p t i e", e=2),
                                             ctx_in[:, t, :].rearrange("p t (i e) -> p t i e", e=2),
                                             rope[:, t, 0, :].unsqueeze(3).to_broadcast([P, 8, 64, 2]), ALU.mult))
                dve.wait_ge(rot_done, 2 * n + 2)
                nc.vector.tensor_tensor(kr[:, n % 2], kr[:, n % 2], kr2[:, n % 2], ALU.add).then_inc(kr_done, 1)

            def rope_low(n):
                t = slice(8 * n, 8 * n + 8)
                dve.wait_ge(vhi_done, n + 1)
                nc.vector.tensor_tensor(vx[:, t, K + 1:VW], kr[:, n % 2], vx[:, t, 0:K], ALU.subtract).then_inc(vlo_done, 1)
                dve.wait_ge(vlo_done, n + 1)
                dve.wait_ge(kthi_done, n + 1)
                nc.vector.tensor_tensor(kt_lo[:, 1024 * n:1024 * n + 1024], psS[0][:, :],
                                        kt_hi[:, 1024 * n:1024 * n + 1024], ALU.subtract).then_inc(ktlo_done, 1)
                if n == 0:
                    dve.wait_ge(wkr_split, 1)
                    nc.vector.tensor_tensor(wkr_lo, wkr_in, wkr_hi, ALU.subtract).then_inc(wkr_split, 1)

            def aux(q, n, step):
                if step[0] == "t":
                    return
                dve.wait_ge(s_aux, q * AUX + n + 1)
                if step[0] == "k":
                    c = slice(512 * step[1], 512 * step[1] + 512)
                    dve.wait_ge(s_khi, q * 8 + step[1] + 1)
                    nc.vector.tensor_tensor(k_lo[:, c], psA[n % 2][:, :], k_hi[:, c], ALU.subtract).then_inc(s_free, 1)
                elif step[0] == "m":
                    _, c, j, st = step
                    nc.vector.reduce_max(maxes[:, TT * j + st, c:c + 1], psA[n % 2][:, :], AX.X).then_inc(s_free, 1)
                if n == LAST_MAX:
                    dve.wait_ge(s_free, q * AUX + n + 1)
                    nc.vector.reduce_max(mx4, maxes, AX.X).then_inc(s_mx, 1)
                    dve.wait_ge(s_mx, q + 1)
                    nc.vector.tensor_scalar_mul(negm, mx4, -1.0).then_inc(s_negm, 1)

            def one_over_sum(p, j):
                hd = p * 2 + j
                dve.wait_ge(s_out, hd * 2 + 2)
                wait(dve, ctx_done, hd)
                nc.vector.reciprocal(rsum, raw[:, :, K]).then_inc(s_rsum, 1)

            def body(p, ahead=True):
                for s in range(SLOTS):
                    t = p * SLOTS + s
                    dve.wait_ge(s_pf, t + 1)
                    wait(dve, s_pv, t - 1)
                    nc.vector.tensor_tensor(p_lo[:, s % 2, :], p_f[:, s % 2, :], p_hi[:, s % 2, :], ALU.subtract).then_inc(s_plo, 1)
                    if s == HALF:
                        one_over_sum(p, 0)
                    if s == 0 and not (isinstance(p, int) and p == 0):
                        one_over_sum(p - 1, 1)
                    if ahead:
                        for n, step in PLAN[s]:
                            aux(p + 1, n, step)
            for what, n, *rest in BEFORE:
                if what == "e":
                    low_query(n)
                elif what == "rope":
                    if n == 0:
                        rope_rows(0)
                    if n < 3:
                        rope_rows(n + 1)
                    rope_low(n)
                elif what == "x":
                    aux(0, n, *rest)
            body(0)
            with dve.Fori(1, NPAIR - 1) as p:
                body(p)
            body(NPAIR - 1, ahead=False)
            one_over_sum(NPAIR - 1, 1)
            for h in range(H):
                dve.wait_ge(lat_mm, h + 1)
                wait(dve, o1_mm, h - 1)
                nc.vector.tensor_copy(latT[:, h % 2, :], psA[h % 2][:, 0:T]).then_inc(lat_copied, 1)
            dve.wait_ge(o1_mm, H)
            for st in range(TT):
                ins = nc.vector.tensor_tensor(x[:, st, :], psO[st][:, :], x[:, st, :], ALU.add)
            ins.then_inc(x1_done, 1)
            dve.wait_ge(x1_done, 1)
            layernorm(2)
            cos2, sin2 = const[:, C_COS:C_COS + T], const[:, C_SIN:C_SIN + T]

            def roped(out_ap, bank, b):
                link(nc.vector.tensor_tensor(out_ap, bank[0:PE2, 0:T], cos2[0:PE2, :], ALU.mult))
                link(nc.vector.tensor_tensor(rope_b[0:PE2, b, :], bank[0:PE2, T:2 * T], sin2[0:PE2, :], ALU.mult))
                return nc.vector.tensor_tensor(out_ap, out_ap, rope_b[0:PE2, b, :], ALU.add)
            dve.wait_ge(kpe_mm, 1)
            roped(qk[0:PE2, 0, T:2 * T], psO[0], 0).then_inc(kpe_done, 1)
            dve.wait_ge(kpe_done, 1)
            scale = float(np.float32(1.0) / np.sqrt(np.float32(QW)))
            for h in range(NH2 + 1):
                if h < NH2:
                    dve.wait_ge(q2_mm, h + 1)
                    wait(dve, s2_mm, h - QK_BUFS + 1)
                    roped(qk[0:PE2, h % QK_BUFS, 0:T], psE[h % 2], h % 2).then_inc(q2_done, 1)
                if h:
                    g = h - 1
                    m = sm[:, g % SM_BUFS, :]
                    dve.wait_ge(s2_mm, h)
                    wait(dve, pT_mm, g - SM_BUFS + 1)
                    link(nc.vector.scalar_tensor_tensor(m, psF[g % 2][:, 0:3 * P], scale, const[:, C_MASK:C_MASK + 3 * P], ALU.mult, ALU.add))
                    nc.vector.tensor_reduce(negm2[:, g, 0:1], m[:, 0:P], AX.X, ALU.max, negate=True)
                    nc.vector.tensor_reduce(negm2[:, g, 1:2], m[:, P:3 * P], AX.X, ALU.max, negate=True).then_inc(s2_max, 1)
            dve.wait_ge(s2_exp, 2 * NH2)
            link(nc.vector.reciprocal(rsum2.rearrange("p s h -> p (s h)"), sums2.rearrange("p s h -> p (s h)")))
            dve.wait_ge(o2_mm, NH2)
            for st in range(TT):
                nc.vector.tensor_tensor(xn[:, st, :].rearrange("p (h v) -> p h v", h=NH2), psO[st][:, :].rearrange("p (h v) -> p h v", h=NH2),
                                        rsum2[:, st, :].unsqueeze(2).to_broadcast([P, NH2, V2]), ALU.mult).then_inc(o2_done, 1)
            dve.wait_ge(x2_mm, 1)
            for st in range(TT):
                ins = nc.vector.tensor_tensor(x[:, st, :], psA[st][:, :], x[:, st, :], ALU.add)
            ins.then_inc(x2_done, 1)
            dve.wait_ge(x2_done, 1)
            layernorm(3)

            def te(i):
                return small[i].rearrange("p (t e) -> p t e", t=TT)

            def first(out_ap, v, width, count, tmp):
                top8, gt, eq, cum, left = tmp
                n = slice(0, width)
                for t in range(TT):
                    link(nc.vector.max(top8[:, t, 0:8], v[:, t, n]))
                for t in range(TT):
                    thr = top8[:, t, count - 1:count]
                    link(nc.vector.tensor_scalar(gt[:, t, n], v[:, t, n], thr, None, ALU.is_gt))
                    link(nc.vector.tensor_scalar(eq[:, t, n], v[:, t, n], thr, None, ALU.is_equal))
                    link(nc.vector.tensor_tensor_scan(cum[:, t, n], ones_e[:, t, n], eq[:, t, n], 0.0, ALU.mult, ALU.add))
                link(nc.vector.reduce_sum(left[:, 0:TT, 0], gt[:, :, n], AX.X))
                link(nc.vector.tensor_scalar(left[:, 0:TT, 1], left[:, 0:TT, 0], -1.0, float(count), ALU.mult, ALU.add))
                for t in range(TT):
                    link(nc.vector.scalar_tensor_tensor(cum[:, t, n], cum[:, t, n], left[:, t, 1:2], eq[:, t, n], ALU.is_le, ALU.mult))
                link(nc.vector.tensor_tensor(out_ap, cum[:, :, n], gt[:, :, n], ALU.add))
            ones_e = te(1)
            link(nc.vector.memset(small[1], 1.0))
            dve.wait_ge(sig_exp, 1)
            dve.wait_ge(ld_bias, 16)
            sc, scb, sel = te(2), te(3), te(4)
            link(nc.vector.tensor_scalar_add(small[0], small[0], 1.0))
            link(nc.vector.reciprocal(small[2], small[0]))
            link(nc.vector.tensor_tensor(scb, sc, bias_e.unsqueeze(1).to_broadcast([P, TT, E]), ALU.add))
            quad = small[3].rearrange("p (g a b) -> p g a b", a=2, b=2)
            s2 = small[5][:, 0:32].rearrange("p (g a) -> p g a", a=2)
            m2 = small[5][:, 32:64].rearrange("p (g a) -> p g a", a=2)
            gs = small[6][:, 0:16]
            link(nc.vector.tensor_tensor(s2, quad[:, :, :, 0], quad[:, :, :, 1], ALU.add))
            link(nc.vector.tensor_tensor(m2, quad[:, :, :, 0], quad[:, :, :, 1], ALU.max))
            link(nc.vector.tensor_tensor(gs, m2[:, :, 0], m2[:, :, 1], ALU.add))
            link(nc.vector.tensor_tensor(small[6][:, 16:32], s2[:, :, 0], s2[:, :, 1], ALU.max))
            link(nc.vector.tensor_tensor(gs, gs, small[6][:, 16:32], ALU.max))
            tmp = [te(7), te(8), te(9), te(10), te(11)]
            gsel = small[6][:, 32:48]
            first(gsel.rearrange("p (t g) -> p t g", t=TT), gs.rearrange("p (t g) -> p t g", t=TT), ROUTE_GROUPS, TOP_GROUPS, tmp)
            link(nc.vector.tensor_tensor(small[12].rearrange("p (g e) -> p g e", g=TT * ROUTE_GROUPS), small[3].rearrange("p (g e) -> p g e", g=TT * ROUTE_GROUPS),
                                         gsel.unsqueeze(2).to_broadcast([P, TT * ROUTE_GROUPS, E // ROUTE_GROUPS]), ALU.mult))
            first(sel, te(12), E, TOP_EXPERTS, tmp)
            nc.vector.tensor_copy(small[13], small[4]).then_inc(sel_done, 1)
            link(nc.vector.tensor_tensor(small[5], small[2], small[4], ALU.mult))
            wsum = small[6][:, 0:2]
            link(nc.vector.reduce_sum(wsum, te(5), AX.X))
            link(nc.vector.tensor_scalar_add(wsum, wsum, 1e-20))
            link(nc.vector.reciprocal(small[6][:, 2:4], wsum))
            for t in range(TT):
                link(nc.vector.tensor_scalar(te(5)[:, t, :], te(5)[:, t, :], small[6][:, 2 + t:3 + t], ROUTE_SCALE, ALU.mult, ALU.mult))
            link(nc.vector.tensor_scalar(small[7], small[4], -1000.0, 1000.0, ALU.mult, ALU.add))
            dve.wait_ge(pos_mm, 1)
            link(nc.vector.tensor_tensor(small[7], psA[1][:, 0:TT * E], small[7], ALU.add))
            dve.wait_ge(cleared, 2)
            slot_of = te(7)
            for t in range(TT):
                nc.vector.tensor_tensor(oh[:, t, :].rearrange("p (e s) -> p e s", e=E), slot_of[:, t, :].unsqueeze(2).to_broadcast([P, E, CAP]),
                                        const[:, C_IOTA:C_IOTA + CAP].unsqueeze(1).to_broadcast([P, E, CAP]), ALU.is_equal).then_inc(oh_done, 1)
            for t in range(TT):
                dve.wait_ge(oh_done, t + 1)
                nc.vector.tensor_tensor(ow[:, t, :, 0:CAP], oh[:, t, :].rearrange("p (e s) -> p e s", e=E),
                                        te(5)[:, t, :].unsqueeze(2).to_broadcast([P, E, CAP]), ALU.mult).then_inc(ow_done, 1)

            def shared_product(i):
                dve.wait_ge(sh_silu, i + 1)
                nc.vector.tensor_tensor(hs[:, i, :], sh_bank[i][:, T:2 * T], hs[:, i, :], ALU.mult).then_inc(sh_done, 1)
            for i in range(SH_EARLY):
                shared_product(i)
            for g in range(NG):
                dve.wait_ge(gu_silu, g + 1)
                nc.vector.tensor_tensor(hid[:, g % 2, :], psF[g % 2][:, FI:2 * FI], hid[:, g % 2, :], ALU.mult).then_inc(hid_done, 1)
                dve.wait_ge(y_mm, g + 1)
                wait(dve, comb_mm, g - 1)
                nc.vector.tensor_copy(y[:, g % 2, :], psA[g % 2][:, :]).then_inc(y_copied, 1)
                if g == 0:
                    for i in range(SH_EARLY, DC):
                        shared_product(i)
            dve.wait_ge(comb_mm, NG)
            for st in range(TT):
                ins = nc.vector.tensor_tensor(x[:, st, :], psO[st][:, :], x[:, st, :], ALU.add)
            ins.then_inc(x3_done, 1)

        @block.tensor
        def _(pe):
            mm = nc.tensor.matmul

            def xn_transposes(n):
                for s in range(TT):
                    pe.wait_ge(ln_xn, TT * (n - 1) + s + 1)
                    for c in range(DC):
                        last = nc.tensor.transpose(psE[s][:, P * c:P * c + P], xn[:, s, P * c:P * c + P], ident)
                    last.then_inc(ln_tr, 1)
            pe.wait_ge(ld_const, 16)
            xn_transposes(1)
            pe.wait_ge(ln_T, 1 * TT)
            def rope_transposes(n):
                pe.wait_ge(kr_done, n + 1)
                wait(pe, ktlo_done, n)
                for i in range(8):
                    last = nc.tensor.transpose(psS[0][:, P * i:P * i + P], kr[:, n % 2, i, :], ident)
                last.then_inc(krT_done, 1)

            def query(what, h, c=0):
                n, j = h // 2, h % 2
                w = w_pair[:, n % PAIR_BUFS, :]
                wq = w[:, 0:DC * 2 * K].rearrange("p (c k) -> p c k", c=DC)
                wk = w[:, DC * 2 * K:DC * 2 * K + 3 * 2 * K].rearrange("p (c k) -> p c k", c=3)
                wr = w[:, DC * 2 * K + 3 * 2 * K:W_PAIR].rearrange("p (c r) -> p c r", c=3)
                if what == "hk":
                    if c == 0:
                        pe.wait_ge(ld_pair[n % PAIR_BUFS], 16 * (n // PAIR_BUFS + 1))
                        wait(pe, qhk_copied, h - 1)
                    last = mm(psO[h % 2][:, 0:T], wq[:, c, K * j:K * j + K], xnT[:, c, :], start=c == 0, stop=c == DC - 1)
                    if c == DC - 1:
                        last.then_inc(qhk_mm, 1)
                elif what == "b":
                    wait(pe, qlo_done, h - 1)
                    wait(pe, qhi_done, h - 1)
                    for c in range(3):
                        last = mm(psF[h % 2][:, 0:R], wk[:, c, K * j:K * j + K], wr[:, c, R * j:R * j + R], start=c == 0, stop=c == 2)
                    last.then_inc(b_mm, 1)
                else:
                    pe.wait_ge(b_copied, h + 1)
                    pe.wait_ge(qhk_copied, h + 1)
                    mm(psF[h % 2][:, T:2 * T], b_dup[:, h % 2, :], qhk[:, h % 2, :], start=True, stop=True).then_inc(q_mm, 1)

            def aux(q, n, step):
                bank = psA[n % 2]
                wait(pe, s_free, q * AUX + n - 1)
                if step[0] == "k":
                    c = slice(512 * step[1], 512 * step[1] + 512)
                    if step[1] == 0:
                        pe.wait_ge(qmax_copied, q * 3 + 3)
                    mm(bank[:, :], wkr_now[:, 0, :], kt_hi[:, c], start=True, stop=False)
                    mm(bank[:, :], wkr_now[:, 0, :], kt_lo[:, c], start=False, stop=False)
                    mm(bank[:, :], wkr_now[:, 1, :], kt_hi[:, c], start=False, stop=True).then_inc(s_aux, 1)
                elif step[0] == "m":
                    _, c, j, st = step
                    if j == 0 and st == 0:
                        pe.wait_ge(s_khi, q * 8 + c + 1)
                    r = slice(R * j, R * j + R)
                    mm(bank[:, :], q_max[r, j, P * st:P * st + P], k_hi[r, 512 * c:512 * c + 512], start=True, stop=True).then_inc(s_aux, 1)
                else:
                    j = step[1]
                    pe.wait_ge(s_negm, q + 1)
                    for st in range(TT):
                        last = mm(bank[R:R + 1, P * st:P * st + P], negm[:, TT * j + st:TT * j + st + 1], ident_b, start=True, stop=True)
                    last.then_inc(s_aux, 1)

            def aux_part(q, s, part):
                for n, step in PLAN[s][part]:
                    aux(q, n, step)

            def scores(p, s):
                if s == SLOTS:
                    p, s = p + 1, 0
                j, g = s // HALF, s % HALF
                wait(pe, s_pf, p * SLOTS + s - 1)
                if g == 0:
                    pe.wait_ge(k_copied[j], p * 80 + 80)
                    pe.wait_ge(s_free, p * AUX + AUX - 1 + j)
                for i in range(GROUP):
                    l = slice(P * (GROUP * g + i), P * (GROUP * g + i) + P)
                    o = psS[s % 2][:, T * i:T * i + T]
                    mm(o, k1[:, j, l], q1[:, j, :], start=True, stop=False)
                    last = mm(o, k2[0:R + 1, j, l], q2[0:R + 1, j, :], start=False, stop=True)
                last.then_inc(s_scores, 1)

            def context_hi(p, s):
                g, t = s % HALF, p * SLOTS + s
                pe.wait_ge(s_phi, t + 1)
                for st in range(TT):
                    if g == 0:
                        wait(pe, s_out, p * 4 + 2 * (s // HALF) - 1 + st)
                    for i in range(GROUP):
                        mm(psO[st][:, 0:VW], p_hi[:, s % 2, T * i + P * st:T * i + P * st + P], vx[:, GROUP * g + i, :],
                           start=g == 0 and i == 0, stop=False)

            def context_lo(p, s):
                g, t = s % HALF, p * SLOTS + s
                pe.wait_ge(s_plo, t + 1)
                for i in range(GROUP):
                    for st in range(TT):
                        last = mm(psO[st][:, 0:K + 1], p_lo[:, s % 2, T * i + P * st:T * i + P * st + P], vx[:, GROUP * g + i, 0:K + 1],
                                  start=False, stop=g == HALF - 1 and i == GROUP - 1)
                last.then_inc(s_pv, 1)

            def body(p, ahead=True):
                for s in range(SLOTS):
                    if s < SLOTS - 1 or ahead:
                        scores(p, s + 1)
                    early = 0 if s == SLOTS - 2 else 1
                    if ahead:
                        aux_part(p + 1, s, slice(0, early))
                    context_hi(p, s)
                    if ahead:
                        aux_part(p + 1, s, slice(early, 2))
                    context_lo(p, s)
                    if ahead:
                        aux_part(p + 1, s, slice(2, None))
            for what, n, *rest in BEFORE:
                if what == "rope":
                    rope_transposes(n)
                elif what != "x":
                    query(what, n, *rest)
                else:
                    if n == 0:
                        pe.wait_ge(ktlo_done, 4)
                        pe.wait_ge(kthi_done, 4)
                        pe.wait_ge(vlo_done, 4)
                        pe.wait_ge(ident_done, 1)
                    aux(0, n, *rest)
            pe.wait_ge(qlo_done, H)
            pe.wait_ge(ones_done, 1)
            scores(0, 0)
            body(0)
            with pe.Fori(1, NPAIR - 1) as p:
                body(p)
            body(NPAIR - 1, ahead=False)
            pe.wait_ge(ctx_done, H)
            pe.wait_ge(s_out, 2 * H)
            pe.wait_ge(ld_wkv, 16)
            pe.wait_ge(ld_wo1, 16)
            for h in range(H + 2):
                if h < H:
                    wait(pe, ct_copied, h - 1)
                    for st in range(TT):
                        last = nc.tensor.transpose(psS[0][:, 512 * (h % 2) + P * st:512 * (h % 2) + P * st + P], ctx_all[:, st, h, :], ident)
                    last.then_inc(ct_mm, 1)
                if 1 <= h <= H:
                    g = h - 1
                    pe.wait_ge(ct_copied, g + 1)
                    wait(pe, lat_copied, g - 1)
                    mm(psA[g % 2][:, 0:T], wkv[:, g, :], ctxT[:, g % 2, :], start=True, stop=True).then_inc(lat_mm, 1)
                if h >= 2:
                    g = h - 2
                    pe.wait_ge(lat_copied, g + 1)
                    for st in range(TT):
                        last = mm(psO[st][:, :], latT[:, g % 2, P * st:P * st + P], wo1[:, g, :], start=g == 0, stop=g == H - 1)
                    last.then_inc(o1_mm, 1)
            xn_transposes(2)
            pe.wait_ge(ln_T, 2 * TT)
            pe.wait_ge(ld_wa, 16)
            pe.wait_ge(lat_copied, H)
            for n, w in enumerate((w_qa, w_kva)):
                for c in range(DC):
                    last = mm(psA[n][:, 0:T], w[:, c, :], xnT[:, c, :], start=c == 0, stop=c == DC - 1)
                last.then_inc(qa_mm, 1)
            pe.wait_ge(x1_done, 1)
            for n, o in ((0, NOPE), (1, 0)):
                for c in range(DC):
                    last = mm(psO[0][0:PE2, T * n:T * n + T], w_kpe[:, c, o:o + PE2], xnT[:, c, :], start=c == 0, stop=c == DC - 1)
            last.then_inc(kpe_mm, 1)
            pe.wait_ge(qa_copied, 2)
            pe.wait_ge(ld_kvb, 16)

            def values():
                for st in range(TT):
                    mm(psA[st][:, :], ckv[:, P * st:P * st + P], w_vb, start=True, stop=True).then_inc(v_mm, 1)

            def queries(h):
                if h == 0:
                    pe.wait_ge(ld_qb, 16)
                wait(pe, q2_done, h - 1)
                wait(pe, qk_copied, h - 1)
                bank = psE[h % 2]
                mm(bank[0:QW, 0:T], w_qb[:, h, NOPE:P], qa, start=True, stop=True)
                mm(bank[0:PE2, T:2 * T], w_qb[:, h, 0:PE2], qa, start=True, stop=True)
                mm(bank[PE2:QW, T:2 * T], w_kb[:, h, :], ckv, start=True, stop=True).then_inc(q2_mm, 1)

            def scores2(h):
                if h == 0:
                    pe.wait_ge(kpe_spread, 1)
                pe.wait_ge(q2_done, h + 1)
                pe.wait_ge(qk_copied, h + 1)
                wait(pe, s2_max, h - 1)
                q, k = qk[0:QW, h % QK_BUFS, 0:T], qk[0:QW, h % QK_BUFS, T:2 * T]
                mm(psF[h % 2][:, 0:P], q[:, 0:P], k[:, 0:P], start=True, stop=True)
                mm(psF[h % 2][:, P:3 * P], q[:, P:T], k, start=True, stop=True).then_inc(s2_mm, 1)

            def transposes2(h):
                if h == 0:
                    pe.wait_ge(v_copied, TT)
                pe.wait_ge(s2_exp, 2 * h + 2)
                wait(pe, pT_copied, h - 1)
                for i in range(3):
                    last = nc.tensor.transpose(psA[h % 2][:, P * i:P * i + P], sm[:, h % SM_BUFS, P * i:P * i + P], ident)
                last.then_inc(pT_mm, 1)

            def values2(h):
                pe.wait_ge(pT_copied, h + 1)
                w = slice(V2 * h, V2 * h + V2)
                mm(psO[0][:, w], pT[:, h % 2, 0:P], v2[:, 0, w], start=True, stop=True)
                mm(psO[1][:, w], pT[:, h % 2, P:2 * P], v2[:, 0, w], start=True, stop=False)
                mm(psO[1][:, w], pT[:, h % 2, 2 * P:3 * P], v2[:, 1, w], start=False, stop=True).then_inc(o2_mm, 1)
            for h in range(NH2 + 5):
                if h < NH2:
                    queries(h)
                if h == 0:
                    values()
                if 0 <= h - 1 < NH2:
                    scores2(h - 1)
                if 0 <= h - 3 < NH2:
                    transposes2(h - 3)
                if 0 <= h - 4 < NH2:
                    values2(h - 4)
            for st in range(TT):
                pe.wait_ge(o2_done, st + 1)
                for c in range(DC):
                    last = nc.tensor.transpose(psS[0][:, T * c + P * st:T * c + P * st + P], xn[:, st, P * c:P * c + P], ident)
            last.then_inc(o2T_mm, 1)
            pe.wait_ge(o2T_copied, 1)
            pe.wait_ge(ld_wo2, 16)
            for st in range(TT):
                for c in range(DC):
                    last = mm(psA[st][:, :], xnT[:, c, P * st:P * st + P], wo2[:, c, :], start=c == 0, stop=c == DC - 1)
            last.then_inc(x2_mm, 1)
            xn_transposes(3)
            pe.wait_ge(ln_T, 3 * TT)
            pe.wait_ge(ld_router, 16)
            for st in range(TT):
                for c in range(DC):
                    last = mm(psA[0][:, E * st:E * st + E], xnT[:, c, P * st:P * st + P], w_router[:, c, :], start=c == 0, stop=c == DC - 1)
            last.then_inc(logit_mm, 1)

            def shared_hidden(i):
                for n, w in enumerate((sg, su)):
                    if i == 0:
                        pe.wait_ge(ld_shared[n], 16)
                    for c in range(DC):
                        last = mm(sh_bank[i][:, T * n:T * n + T], w[:, c, P * i:P * i + P], xnT[:, c, :], start=c == 0, stop=c == DC - 1)
                last.then_inc(sh_mm, 1)

            def shared_out(i):
                if i == 0:
                    pe.wait_ge(ld_shared[2], 16)
                pe.wait_ge(sh_done, i + 1)
                for st in range(TT):
                    mm(psO[st][:, :], hs[:, i, P * st:P * st + P], sd[:, i, :], start=False, stop=False)
            for i in range(SH_EARLY):
                shared_hidden(i)
            pe.wait_ge(sel_done, 1)
            early, ones = const[:, C_EARLY:C_EARLY + P], const[:, C_ONES:C_ONES + P]
            chosen = small[13].rearrange("p (t e) -> p t e", t=TT)
            mm(psA[1][:, 0:E], early, chosen[:, 0, :], start=True, stop=True)
            mm(psA[1][:, E:2 * E], ones, chosen[:, 0, :], start=True, stop=False)
            mm(psA[1][:, E:2 * E], early, chosen[:, 1, :], start=False, stop=True).then_inc(pos_mm, 1)
            pe.wait_ge(oh_done, TT)
            pe.wait_ge(cleared, 2)
            for c in range(DC):
                wait(pe, xp_copied, c - 1)
                for st in range(TT):
                    last = mm(psE[c % 2][:, 0:E * CAP], xn[:, st, P * c:P * c + P], oh[:, st, :], start=st == 0, stop=st == TT - 1)
                last.then_inc(xp_mm, 1)

            def weights_by_slot():
                pe.wait_ge(ow_done, TT)
                for i in range(NG // 2):
                    wait(pe, owT_copied, i - 1)
                    for n in range(2):
                        for st in range(TT):
                            o = T * n + P * st
                            last = nc.tensor.transpose(psA[i % 2][:, o:o + P], ow[:, st, GE * (2 * i + n):GE * (2 * i + n + 1), :].rearrange("p e s -> p (e s)"), ident)
                    last.then_inc(owT_mm, 1)
            pe.wait_ge(xp_copied, DC)

            def gate_up(g):
                pe.wait_ge(sh_done, min(g, 1) + 1)
                wait(pe, hid_done, g - 1)
                for j in range(GE):
                    e = GE * g + j
                    pe.wait_ge(ld_gu[e % RING], 16 * (e // RING + 1))
                for c in range(DC):
                    for j in range(GE):
                        e = GE * g + j
                        last = mm(psF[g % 2][SLOT * j:SLOT * j + SLOT, :], xpT[:, c, CAP * e:CAP * e + SLOT], ring[e % RING][:, 2 * FI * c:2 * FI * (c + 1)],
                                  start=c == 0, stop=c == DC - 1)
                last.then_inc(gu_mm, 1)

            def down(g):
                pe.wait_ge(hid_done, g + 1)
                wait(pe, hT_copied, g - 1)
                for c in range(FC):
                    last = nc.tensor.transpose(psE[g % 2][:, P * c:P * c + P], hid[:, g % 2, P * c:P * c + P], ident)
                last.then_inc(hT_mm, 1)
                pe.wait_ge(hT_copied, g + 1)
                wait(pe, y_copied, g - 1)
                if g < 2:
                    pe.wait_ge(owT_copied, NG // 2)
                for j in range(GE):
                    e = GE * g + j
                    pe.wait_ge(ld_down[e % RING], 16 * (e // RING + 1))
                for c in range(FC):
                    for j in range(GE):
                        e = GE * g + j
                        o = 2 * FI * DC + D * c
                        last = mm(psA[g % 2][SLOT * j:SLOT * j + SLOT, :], hT[:, g % 2, c, SLOT * j:SLOT * j + SLOT], ring[e % RING][:, o:o + D],
                                  start=c == 0, stop=c == FC - 1)
                last.then_inc(y_mm, 1)

            def combine(g):
                if g == 0:
                    pe.wait_ge(sh_done, DC)
                pe.wait_ge(y_copied, g + 1)
                for st in range(TT):
                    last = mm(psO[st][:, :], owT[:, g, P * st:P * st + P], y[:, g % 2, :], start=g == 0, stop=g == NG - 1)
                last.then_inc(comb_mm, 1)
            for g in range(NG):
                gate_up(g)
                if g == 0:
                    weights_by_slot()
                else:
                    combine(g - 1)
                down(g)
                if g == 0:
                    for i in range(SH_EARLY, DC):
                        shared_hidden(i)
                elif g <= DC:
                    shared_out(g - 1)
            combine(NG - 1)


def constants():
    c = np.zeros((P, C_END), np.float32)
    i = np.arange(P)
    c[:, C_ID:C_ID + P] = np.eye(P)
    causal = np.where(i[:, None] >= i[None, :], 0, NEG)
    c[:, C_MASK:C_MASK + P] = causal
    c[:, C_MASK + 2 * P:C_MASK + 3 * P] = causal
    c[:, C_EARLY:C_EARLY + P] = i[:, None] < i[None, :]
    c[:, C_ONES:C_ONES + P] = 1
    c[:, C_IOTA:C_IOTA + 16] = np.arange(16)
    inv = (np.float32(10000.0) ** (-np.arange(0, 64, 2, dtype=np.float32) / np.float32(64))).astype(np.float32)
    ang = (np.arange(T, dtype=np.float32)[:, None] * inv[None, :]).astype(np.float32)
    c[0:32, C_COS:C_COS + T] = c[32:64, C_COS:C_COS + T] = np.cos(ang).T
    c[64:96, C_COS:C_COS + T] = 1
    c[0:32, C_SIN:C_SIN + T] = -np.sin(ang).T
    c[32:64, C_SIN:C_SIN + T] = np.sin(ang).T
    inv = (np.float32(1.0) / np.float32(10000.0) ** (np.arange(0, K, 2, dtype=np.float32) / np.float32(K))).astype(np.float32)
    ang = (np.arange(L, dtype=np.float32)[:, None] * inv[None, :]).astype(np.float32)
    sin = np.sin(ang)
    sin[:, 0:32] *= -1
    rope = np.stack([np.cos(ang), sin], 1).reshape(LT, P, 2, 64).transpose(1, 0, 2, 3)
    return c, np.ascontiguousarray(rope, np.float32)


def rows(w, parts=P):
    return np.asarray(w).reshape(-1, parts, w.shape[1]).transpose(1, 0, 2)


def lay_out(i):
    g = {k: np.asarray(v) for k, v in i.items()}
    const, rope = constants()
    arrays = {"x": g["x"], "const": const, "rope": rope}
    arrays["ctx"] = g["ctx_512"].reshape(LT, P, K).transpose(1, 0, 2)
    wq = rows(g["L0_xattn_Wq"].T)
    wk = g["L0_xattn_w_kc_q"].transpose(2, 0, 1).reshape(3, P, H, K).transpose(1, 0, 2, 3)
    wr = g["L0_xattn_W_qr"].transpose(1, 0, 2).reshape(3, P, H, R).transpose(1, 0, 2, 3)
    arrays["w_pair"] = np.stack([np.concatenate([
        wq[:, :, 2 * K * n:2 * K * n + 2 * K].reshape(P, -1),
        wk[:, :, 2 * n:2 * n + 2].reshape(P, -1), wr[:, :, 2 * n:2 * n + 2].reshape(P, -1)], 1) for n in range(NPAIR)])
    arrays["w_kr"] = g["L0_xattn_W_kr"].transpose(1, 0, 2).reshape(P, H * R)
    arrays["w_kv"] = g["L0_xattn_w_kc_kv"].transpose(2, 0, 1)
    arrays["w_o1"] = rows(g["L0_xattn_Wo"].T)
    kva = g["L0_attn_Wkva"]
    kpe = kva[:, P:]
    even, odd = kpe[:, 0::2], kpe[:, 1::2]
    arrays["w_a"] = np.concatenate([rows(g["L0_attn_Wqa"]).reshape(P, -1), rows(kva[:, :P]).reshape(P, -1),
                                    rows(np.concatenate([odd, even, odd], 1)).reshape(P, -1)], 1)
    qb = g["L0_attn_Wqb"].reshape(P, NH2, QW)
    pe = qb[:, :, NOPE:]
    arrays["w_qb"] = np.concatenate([pe[:, :, 1::2], pe[:, :, 0::2], pe[:, :, 1::2], qb[:, :, :NOPE]], 2)
    kvb = g["L0_attn_Wkvb"].reshape(P, NH2, NOPE + V2)
    arrays["w_kvb"] = np.concatenate([kvb[:, :, :NOPE].reshape(P, -1), kvb[:, :, NOPE:].reshape(P, -1)], 1)
    arrays["w_o2"] = rows(g["L0_attn_Wo"])
    arrays["w_router"] = rows(g["L0_ffn_router_w"].T)
    arrays["e_bias"] = g["L0_ffn_e_bias"]
    arrays["w_shared"] = np.stack([rows(g[f"L0_ffn_shared_{n}"].T) for n in ("gate", "up", "down")])
    up = [g[f"L0_ffn_W_{n}"].reshape(E, DC, P, FI) for n in ("gate", "up")]
    down = g["L0_ffn_W_down"].reshape(E, FC, P, D).transpose(0, 2, 1, 3).reshape(E, P, -1)
    arrays["w_exp"] = np.concatenate([np.concatenate(up, 3).transpose(0, 2, 1, 3).reshape(E, P, -1), down], 2)
    return {k: np.ascontiguousarray(v) for k, v in arrays.items()}


def kernel(**inputs):
    import concourse.bacc as bacc
    from concourse.bass_utils import run_bass_kernel_spmd

    nc = bacc.Bacc("TRN2", target_bir_lowering=False, num_devices=1)
    arrays = lay_out(inputs)
    aps = {n: nc.dram_tensor(n, v.shape, F32, kind="ExternalInput").ap() for n, v in arrays.items()}
    out = nc.dram_tensor("out", (1, T, D), F32, kind="ExternalOutput").ap()
    layer(nc, aps, out)
    r = run_bass_kernel_spmd(nc, [arrays], core_ids=[0])
    return r.results[0]["out"]
```
